# Optimizing a Trainium2 kernel written in Bass

```python
import numpy as np
import jax
import jax.numpy as jnp

def _softmax(x, axis=-1):
    return jax.nn.softmax(x, axis=axis)
def _gelu(x):
    return jax.nn.gelu(x, approximate=True)
def _silu(x):
    return jax.nn.silu(x)
def _sigmoid(x):
    return jax.nn.sigmoid(x)
def _layernorm(x, axis=-1, eps=1e-5):
    m = jnp.mean(x, axis=axis, keepdims=True)
    v = jnp.var(x, axis=axis, keepdims=True)
    return (x - m) / jnp.sqrt(v + eps)
def _scatter_add(tgt, idx, src, axis=0):
    return tgt.at[idx].add(src)
def _segment_sum(src, seg, n):
    return jax.ops.segment_sum(src, seg, n)

kernel_name = 'mk_conv_preact_d2_conv_nhwc256_f69d02'

def setup_inputs(seed: int = 0):
    np.random.seed(seed)
    _w = jnp.asarray
    def _rec_inputs():
        import jax
        import jax.numpy as jnp
        _gk = jax.random.key(seed)
        x = 7.22e-05 + 1 * jax.random.normal(jax.random.fold_in(_gk, 1), (8, 64, 64, 256), jnp.float32)
        return x
    x = _rec_inputs()
    def _L0_conv_setup():
        import jax, jax.numpy as jnp
        import numpy as np
        N, H, W, C = (8, 64, 64, 256)
        GC = 8
        G = C // GC
        K = 3
        KK = K * K
        DK = 3

        def _dcnv4(x, dw_w, dw_b, om_w, om_b, vp_w, vp_b, op_w):
            n, h, w, c = x.shape
            xdw = jax.lax.conv_general_dilated(x, dw_w, window_strides=(1, 1), padding='SAME', dimension_numbers=('NHWC', 'HWIO', 'NHWC'), feature_group_count=c) + dw_b
            om = (xdw @ om_w + om_b).reshape(n, h, w, G, KK * 3)
            offset = om[..., :2 * KK].reshape(n, h, w, G, KK, 2)
            mask = om[..., 2 * KK:]
            value = (x @ vp_w + vp_b).reshape(n, h, w, G, GC)
            kg = (jnp.arange(K) - (K - 1) // 2).astype(jnp.float32)
            ky = jnp.repeat(kg, K)
            kx = jnp.tile(kg, K)
            base_y = jnp.arange(h, dtype=jnp.float32).reshape(1, h, 1, 1, 1)
            base_x = jnp.arange(w, dtype=jnp.float32).reshape(1, 1, w, 1, 1)
            py = base_y + ky + offset[..., 1]
            px = base_x + kx + offset[..., 0]
            y0 = jnp.floor(py)
            x0 = jnp.floor(px)
            ty = py - y0
            tx = px - x0
            n_idx = jnp.arange(n).reshape(n, 1, 1, 1, 1)
            g_idx = jnp.arange(G).reshape(1, 1, 1, G, 1)

            def gather(yi, xi):
                valid = (yi >= 0) & (yi <= h - 1) & (xi >= 0) & (xi <= w - 1)
                yc = jnp.clip(yi, 0, h - 1).astype(jnp.int32)
                xc = jnp.clip(xi, 0, w - 1).astype(jnp.int32)
                v = value[n_idx, yc, xc, g_idx]
                return v * valid[..., None].astype(value.dtype)
            v00 = gather(y0, x0)
            v01 = gather(y0, x0 + 1)
            v10 = gather(y0 + 1, x0)
            v11 = gather(y0 + 1, x0 + 1)
            sampled = ((1 - ty) * (1 - tx))[..., None] * v00 + ((1 - ty) * tx)[..., None] * v01 + (ty * (1 - tx))[..., None] * v10 + (ty * tx)[..., None] * v11
            out = jnp.einsum('nhwgkc,nhwgk->nhwgc', sampled, mask).reshape(n, h, w, c)
            return out @ op_w
        key = jax.random.key(seed)
        ks = jax.random.split(key, 6)
        s = 0.02
        return {'x': jax.random.normal(ks[0], (N, H, W, C), jnp.float32), 'dw_w': jax.random.normal(ks[1], (DK, DK, 1, C), jnp.float32) * s, 'dw_b': jnp.zeros((C,), jnp.float32), 'om_w': jax.random.normal(ks[2], (C, G * KK * 3), jnp.float32) * s, 'om_b': jnp.zeros((G * KK * 3,), jnp.float32), 'vp_w': jax.random.normal(ks[3], (C, C), jnp.float32) * s, 'vp_b': jnp.zeros((C,), jnp.float32), 'op_w': jax.random.normal(ks[4], (C, C), jnp.float32) * s}
    _L0_conv_all = _L0_conv_setup()
    _L0_conv_in = {k: v for k, v in _L0_conv_all.items() if k in ('dw_w', 'dw_b', 'om_w', 'om_b', 'vp_w', 'vp_b', 'op_w', )}
    del _L0_conv_all

    def _L1_conv_setup():
        import jax, jax.numpy as jnp
        import numpy as np
        from jax import lax
        KH, KW, PAD = (3, 3, 1)

        def _sign_pm1(v):
            return jnp.where(v > 0, jnp.float32(1.0), jnp.float32(-1.0)).astype(v.dtype)
        key = jax.random.key(seed)
        k1, k2, k3 = jax.random.split(key, 3)
        x = jax.random.normal(k1, (32, 56, 56, 256), dtype=jnp.float32)
        kernel = jax.random.normal(k2, (KH, KW, 256, 256), dtype=jnp.float32) * 0.05
        bias = jax.random.normal(k3, (256,), dtype=jnp.float32) * 0.01
        return {'x': x, 'kernel': kernel, 'bias': bias}
    _L1_conv_all = _L1_conv_setup()
    _L1_conv_in = {k: v for k, v in _L1_conv_all.items() if k in ('kernel', 'bias', )}
    del _L1_conv_all

    return {
        "x": x,
        "L0_conv_dw_w": _L0_conv_in["dw_w"],
        "L0_conv_dw_b": _L0_conv_in["dw_b"],
        "L0_conv_om_w": _L0_conv_in["om_w"],
        "L0_conv_om_b": _L0_conv_in["om_b"],
        "L0_conv_vp_w": _L0_conv_in["vp_w"],
        "L0_conv_vp_b": _L0_conv_in["vp_b"],
        "L0_conv_op_w": _L0_conv_in["op_w"],
        "L1_conv_kernel": _L1_conv_in["kernel"],
        "L1_conv_bias": _L1_conv_in["bias"],
    }

def reference(x, L0_conv_dw_w, L0_conv_dw_b, L0_conv_om_w, L0_conv_om_b, L0_conv_vp_w, L0_conv_vp_b, L0_conv_op_w, L1_conv_kernel, L1_conv_bias):
    import jax
    import jax.numpy as jnp
    def _L0_conv_ref(x, dw_w, dw_b, om_w, om_b, vp_w, vp_b, op_w):
        import jax, jax.numpy as jnp
        import numpy as np
        N, H, W, C = (8, 64, 64, 256)
        GC = 8
        G = C // GC
        K = 3
        KK = K * K
        DK = 3

        def _dcnv4(x, dw_w, dw_b, om_w, om_b, vp_w, vp_b, op_w):
            n, h, w, c = x.shape
            xdw = jax.lax.conv_general_dilated(x, dw_w, window_strides=(1, 1), padding='SAME', dimension_numbers=('NHWC', 'HWIO', 'NHWC'), feature_group_count=c) + dw_b
            om = (xdw @ om_w + om_b).reshape(n, h, w, G, KK * 3)
            offset = om[..., :2 * KK].reshape(n, h, w, G, KK, 2)
            mask = om[..., 2 * KK:]
            value = (x @ vp_w + vp_b).reshape(n, h, w, G, GC)
            kg = (jnp.arange(K) - (K - 1) // 2).astype(jnp.float32)
            ky = jnp.repeat(kg, K)
            kx = jnp.tile(kg, K)
            base_y = jnp.arange(h, dtype=jnp.float32).reshape(1, h, 1, 1, 1)
            base_x = jnp.arange(w, dtype=jnp.float32).reshape(1, 1, w, 1, 1)
            py = base_y + ky + offset[..., 1]
            px = base_x + kx + offset[..., 0]
            y0 = jnp.floor(py)
            x0 = jnp.floor(px)
            ty = py - y0
            tx = px - x0
            n_idx = jnp.arange(n).reshape(n, 1, 1, 1, 1)
            g_idx = jnp.arange(G).reshape(1, 1, 1, G, 1)

            def gather(yi, xi):
                valid = (yi >= 0) & (yi <= h - 1) & (xi >= 0) & (xi <= w - 1)
                yc = jnp.clip(yi, 0, h - 1).astype(jnp.int32)
                xc = jnp.clip(xi, 0, w - 1).astype(jnp.int32)
                v = value[n_idx, yc, xc, g_idx]
                return v * valid[..., None].astype(value.dtype)
            v00 = gather(y0, x0)
            v01 = gather(y0, x0 + 1)
            v10 = gather(y0 + 1, x0)
            v11 = gather(y0 + 1, x0 + 1)
            sampled = ((1 - ty) * (1 - tx))[..., None] * v00 + ((1 - ty) * tx)[..., None] * v01 + (ty * (1 - tx))[..., None] * v10 + (ty * tx)[..., None] * v11
            out = jnp.einsum('nhwgkc,nhwgk->nhwgc', sampled, mask).reshape(n, h, w, c)
            return out @ op_w
        return _dcnv4(x, dw_w, dw_b, om_w, om_b, vp_w, vp_b, op_w)

    def _L1_conv_ref(x, kernel, bias):
        import jax, jax.numpy as jnp
        import numpy as np
        from jax import lax
        KH, KW, PAD = (3, 3, 1)

        def _sign_pm1(v):
            return jnp.where(v > 0, jnp.float32(1.0), jnp.float32(-1.0)).astype(v.dtype)
        xp = jnp.pad(x, ((0, 0), (PAD, PAD), (PAD, PAD), (0, 0)))
        bin_k = _sign_pm1(kernel)
        alpha = jnp.mean(jnp.abs(kernel), axis=(0, 1, 2))
        bin_x = _sign_pm1(xp)
        beta = jnp.mean(jnp.abs(xp), axis=3, keepdims=True)
        K = lax.reduce_window(beta, jnp.float32(0.0), lax.add, (1, KH, KW, 1), (1, 1, 1, 1), 'VALID') / (KH * KW)
        Ka = K * alpha
        conv = lax.conv_general_dilated(bin_x, bin_k, window_strides=(1, 1), padding='VALID', dimension_numbers=('NHWC', 'HWIO', 'NHWC'))
        return conv * Ka + bias

    def _gn(v, G=32, eps=1e-5):
        B_, H_, W_, C_ = v.shape
        g = v.reshape(B_, H_, W_, G, C_ // G)
        m = jnp.mean(g, axis=(1, 2, 4), keepdims=True)
        s = jnp.var(g, axis=(1, 2, 4), keepdims=True)
        return ((g - m) / jnp.sqrt(s + eps)).reshape(v.shape)

    def _ln_c(v, eps=1e-6):
        m = jnp.mean(v, axis=-1, keepdims=True)
        s = jnp.var(v, axis=-1, keepdims=True)
        return (v - m) / jnp.sqrt(s + eps)

    def _ln_t(v, eps=1e-5):
        m = jnp.mean(v, axis=-1, keepdims=True)
        s = jnp.var(v, axis=-1, keepdims=True)
        return (v - m) / jnp.sqrt(s + eps)

    def _to_tokens(v):
        B_, H_, W_, C_ = v.shape
        return v.reshape(B_, H_ * W_, C_)
    def _from_tokens(t, like):
        return t.reshape(like.shape)

    x = x + _L0_conv_ref(_gn(x), L0_conv_dw_w, L0_conv_dw_b, L0_conv_om_w, L0_conv_om_b, L0_conv_vp_w, L0_conv_vp_b, L0_conv_op_w)
    x = x + _L1_conv_ref(_gn(x), L1_conv_kernel, L1_conv_bias)
    return x


_drawn_inputs = setup_inputs


def setup_inputs(seed=0):
    import zlib

    import numpy as np

    out = dict(_drawn_inputs(seed))
    spreads = {'L0_conv_dw_b': (0.0, 0.1), 'L0_conv_om_b': (0.0, 0.1), 'L0_conv_vp_b': (0.0, 0.1)}
    factors = {'L1_conv_bias': 8.0}
    for name, (base, spread) in spreads.items():
        noise = np.random.default_rng([zlib.crc32(name.encode()), seed]).standard_normal(out[name].shape)
        drawn = base * np.exp(spread * noise) if base else spread * noise
        out[name] = jnp.asarray(drawn.astype(out[name].dtype))
    for name, factor in factors.items():
        out[name] = (out[name] * factor).astype(out[name].dtype)
    return out
```

```python
from contextlib import ExitStack

import concourse.bass as bass
import numpy as np
from concourse import mybir

F32 = mybir.dt.float32
BF16 = mybir.dt.bfloat16
ALU = mybir.AluOpType
ACT = mybir.ActivationFunctionType
AX_X = mybir.AxisListType.X

P = 128
H = W = 64
HW = H * W
C = 256
CH = C // P
G, GC = 32, 8
TAPS = 9
Q = P // G
QR = H // Q
SR = 4
STEPS = QR // SR
TOK = SR * W
WR = SR + 4
VR, VW = QR + 4, W + 4
D5 = 5
SHIFTS = D5 * D5
C_PE, C_DVE, C_POOL = 2, 3, 3
C_V = C_PE + C_DVE
PBUF = 3
DW_UNITS = 4
V_UNITS = GC // 2
BG_IMG = STEPS * DW_UNITS + (STEPS + 1) * V_UNITS
GROUP = C // 32
FARTHEST = H - 1
EPS = 1e-5


def at_least(eng, sem, value):
    if not isinstance(value, int) or value > 0:
        eng.wait_ge(sem, value)


def bg_before(n, j):
    return n * BG_IMG + (0 if j == 0 else j * (DW_UNITS + V_UNITS) + V_UNITS)


def row_groups(j):
    return [0, 1] if j == 0 else [j + 1]


def layer0_stats(nc, x, consts, tables, NI):
    with ExitStack() as ctx:
        sb = lambda name, shape, dt=F32: ctx.enter_context(nc.sbuf_tensor(name, shape, dt))
        sem = lambda name: ctx.enter_context(nc.semaphore(name))
        xt = sb("st_x", [P, CH, HW])
        bs = sb("st_bs", [P, CH, HW // 512, 6])
        bs_all = sb("st_bs_all", [P, NI, CH * HW // 512 * 6])
        mv = sb("st_mv", [P, NI, CH, 2])
        x_loaded = [sem(f"st_loaded{h}") for h in range(CH)]
        half_summed = [sem(f"st_summed{h}") for h in range(CH)]
        kept, aggregated = sem("st_kept"), sem("st_aggregated")
        with nc.Block() as block:
            @block.sync
            def _(sp):
                def image(n):
                    for h in range(CH):
                        at_least(sp, half_summed[h], n)
                        src = x[bass.ds(n, 1)].rearrange("n (h p) t -> (n h) p t", p=P)
                        sp.dma_start(xt[:, h, :], src[h]).then_inc(x_loaded[h], 16)

                image(0)
                with sp.Fori(1, NI) as n:
                    image(n)

            @block.vector
            def _(dve):
                def image(n):
                    for h in range(CH):
                        dve.wait_ge(x_loaded[h], (n + 1) * 16)
                        if h == 0:
                            at_least(dve, kept, n)
                        for i in range(HW // 512):
                            last = nc.vector.bn_stats(bs[:, h, i, :], xt[:, h, 512 * i:512 * i + 512])
                        last.then_inc(half_summed[h], 1)
                    for h in range(CH):
                        dve.wait_ge(half_summed[h], n + 1)
                    nc.vector.tensor_scalar(bs_all[:, bass.ds(n, 1), :].rearrange("p n s -> p (n s)"),
                                            bs[:, :, :, :].rearrange("p h i s -> p (h i s)"), 1.0, None,
                                            ALU.mult).then_inc(kept, 1)

                image(0)
                with dve.Fori(1, NI) as n:
                    image(n)
                dve.wait_ge(kept, NI)
                for n in range(NI):
                    for h in range(CH):
                        sums = bs_all[:, n, :].rearrange("p (h i s) -> p h i s", h=CH, s=6)[:, h]
                        nc.vector.bn_aggr(mv[:, n, h, :], sums).then_inc(aggregated, 1)
                dve.wait_ge(aggregated, NI * CH)
        group_tables(nc, mv, consts, tables, NI, "gt1_")


def group_tables(nc, mv, consts, tables, NI, u):
    NS = NI * CH
    with ExitStack() as ctx:
        sb = lambda name, shape, dt=F32: ctx.enter_context(nc.sbuf_tensor(name, shape, dt))
        sem = lambda name: ctx.enter_context(nc.semaphore(name))
        mean = sb(u + "mean", [P, NS])
        var = sb(u + "var", [P, NS])
        ps = ctx.enter_context(nc.psum_tensor(u + "ps", [P, 2, 512], F32))
        v, pe_done, act_done = sem(u + "v"), sem(u + "pe"), sem(u + "act")
        with nc.Block() as block:
            @block.vector
            def _(dve):
                dve_steps = [0]

                def after(ins):
                    dve_steps[0] += 1
                    ins.then_inc(v, 1)
                    dve.wait_ge(v, dve_steps[0])

                flat = mv[:, :, :, :].rearrange("p n h s -> p (n h) s")
                after(nc.vector.tensor_copy(mean[:, :], flat[:, :, 0]))
                dve.wait_ge(pe_done, 1)
                gm = tables[:, 2, :]
                after(nc.vector.tensor_copy(gm, ps[:, 0, 0:NS]))
                after(nc.vector.tensor_tensor(mean[:, :], mean[:, :], gm, ALU.subtract))
                after(nc.vector.tensor_tensor(mean[:, :], mean[:, :], mean[:, :], ALU.mult))
                after(nc.vector.tensor_tensor(var[:, :], flat[:, :, 1], mean[:, :], ALU.add))
                dve.wait_ge(pe_done, 2)
                after(nc.vector.tensor_scalar(var[:, :], ps[:, 1, 0:NS], EPS, None, ALU.add))
                dve.wait_ge(act_done, 1)
                after(nc.vector.reciprocal(tables[:, 0, :], var[:, :]))
                after(nc.vector.scalar_tensor_tensor(out=tables[:, 1, :], in0=gm, scalar=-1.0,
                                                     in1=tables[:, 0, :], op0=ALU.mult, op1=ALU.mult))

            @block.tensor
            def _(pe):
                pe.wait_ge(v, 1)
                nc.tensor.matmul(ps[:, 0, 0:NS], consts["mean8"][:, :], mean[:, :],
                                 start=True, stop=True).then_inc(pe_done, 1)
                pe.wait_ge(v, 5)
                nc.tensor.matmul(ps[:, 1, 0:NS], consts["mean8"][:, :], var[:, :],
                                 start=True, stop=True).then_inc(pe_done, 1)

            @block.scalar
            def _(act):
                act.wait_ge(v, 6)
                nc.scalar.activation(var[:, :], var[:, :], ACT.Sqrt).then_inc(act_done, 1)


def tap_rects(ky, kx):
    if ky == 0 and kx == 0:
        return [(0, 3, 0, 3)], []
    if ky == 0:
        return [(0, 3, 2, 3)], [(0, 3, 0, 2)]
    if kx == 0:
        return [(2, 3, 0, 3)], [(0, 2, 0, 3)]
    return [(2, 3, 2, 3)], [(0, 2, 0, 3), (2, 3, 0, 2)]


def layer0(nc, x, zeros, w_dram, x2, consts, tables, mv2, reach, NI):
    with ExitStack() as ctx:
        sb = lambda name, shape, dt=F32: ctx.enter_context(nc.sbuf_tensor(name, shape, dt))
        psum = lambda name, shape: ctx.enter_context(nc.psum_tensor(name, shape, F32))
        sem = lambda name: ctx.enter_context(nc.semaphore(name))

        win = sb("win", [P, CH, Q, WR, W])
        xdw = sb("xdw", [P, CH, Q, TOK])
        val = sb("val", [P, GC, VR, VW])
        hat = sb("hat", [P, 2, 2, 3, TOK])
        msk = sb("msk", [P, 2, TOK])
        over = sb("over", [P, 2, TOK], BF16)
        over_sum = sb("over_sum", [P, 2, TAPS])
        over_max = sb("over_max", [P, 1])
        mwy = sb("mwy", [P, 3, TOK])
        prod = sb("prod", [P, 3, 3, TOK])
        wsum = sb("wsum", [P, 2, D5, D5, TOK])
        pv = sb("pv", [P, PBUF, C_V, TOK])
        pp = sb("pp", [P, C_POOL, TOK])
        acc = sb("acc", [P, GC, TOK])
        acc_t = sb("acc_t", [P, CH, Q * TOK])
        xres = sb("xres", [P, CH, Q, TOK])
        diag = sb("diag", [P, CH, TAPS, P])
        omw = sb("omw", [P, CH, 27, G])
        vpw = sb("vpw", [P, CH, GC, G])
        opw = sb("opw", [P, CH, C])
        dww = sb("dww", [P, CH, TAPS])
        dwb = sb("dwb", [P, CH])
        omb = sb("omb", [P, 27])
        nomb = sb("nomb", [P, 27])
        vpb = sb("vpb", [P, GC])
        mv_now = sb("mv_now", [P, CH, 2])
        gn = sb("gn", [P, 2, 2, CH])
        bs2 = sb("bs2", [P, CH, STEPS * 2, 6])

        ps_xy = psum("ps_xy", [P, 2, 2, TOK])
        ps_m = psum("ps_m", [P, 2, TOK])
        ps_bg = psum("ps_bg", [P, 2, 512])
        ps_add = psum("ps_add", [P, C_PE, TOK])
        ps_pj = psum("ps_pj", [P, 2, 512])

        weights_loaded, diag_made, val_zero = sem("weights_loaded"), sem("diag_made"), sem("val_zero")
        win_loaded, win_normed = sem("win_loaded"), sem("win_normed")
        bg_full, bg_free = sem("bg_full"), sem("bg_free")
        om_full, om_free, msk_free = sem("om_full"), sem("om_free"), sem("msk_free")
        abs_done, w0_done, hat_full = sem("abs_done"), sem("w0_done"), sem("hat_full")
        mwy_done, prod_done, wadd_done = sem("mwy_done"), sem("prod_done"), sem("wadd_done")
        pv_full, add_done, add_out = sem("pv_full"), sem("add_done"), sem("add_out")
        vadd_done, pmul_done, padd_done = sem("vadd_done"), sem("pmul_done"), sem("padd_done")
        acc_sent, xres_loaded = sem("acc_sent"), sem("xres_loaded")
        pj_full, pj_added, stats2 = sem("pj_full"), sem("pj_added"), sem("stats2")
        gn_kept = sem("gn_kept")
        x2_stored, over_done, aggr2 = sem("x2_stored"), sem("over_done"), sem("aggr2")
        mv_kept = sem("mv_kept")
        WL = 16 * 9

        def steps_of_images(eng, step, images_first):
            for j in range(STEPS):
                step(0, j, j == 0, False)
            if NI > 2:
                with eng.Fori(1, NI - 1) as n:
                    for j in range(STEPS):
                        step(n, j, False, False)
            for j in range(STEPS):
                step(NI - 1, j, False, j == STEPS - 1)

        def following(n, j):
            return (n, j + 1) if j < STEPS - 1 else (n + 1, 0)

        def previous(n, j):
            return (n, j - 1) if j > 0 else (n - 1, STEPS - 1)

        x_v = x.rearrange("n (h p) (r w) -> n p h r w", p=P, w=W)
        x2_v = x2.rearrange("n (h p) (r w) -> n p h r w", p=P, w=W)

        def image(v, n):
            return v[n] if isinstance(n, int) else v[bass.ds(n, 1)].rearrange("n p h r w -> p (n h) r w")

        def window_edge(q, j):
            lo = QR * q + SR * j - 2
            return max(0, -lo), WR - max(0, lo + WR - H)

        with nc.Block() as block:
            @block.sync
            def _(sp):
                for dst, name in ((dww, "dww"), (dwb, "dwb"), (omw, "omw"), (omb, "omb"), (vpw, "vpw"),
                                  (vpb, "vpb"), (opw, "opw")):
                    sp.dma_start(dst[:], w_dram[name]).then_inc(weights_loaded, 16)
                sp.dma_start(consts["ident"][:, :], w_dram["ident"]).then_inc(weights_loaded, 16)
                sp.dma_start(consts["spare"][:, :], w_dram["ident"][:, 0:8]).then_inc(weights_loaded, 16)

                def load_window(n, j):
                    at_least(sp, bg_full, bg_before(n, j))
                    for q in range(Q):
                        lo, hi = window_edge(q, j)
                        r0 = QR * q + SR * j - 2
                        sp.dma_start(win[:, :, q, lo:hi, :], image(x_v, n)[:, :, r0 + lo:r0 + hi, :])\
                            .then_inc(win_loaded, 16)
                    for q in (0, Q - 1):
                        lo, hi = window_edge(q, j)
                        if q == 0 and j == 0:
                            sp.dma_start(win[:, :, q, 0:2, :], zeros).then_inc(win_loaded, 16)
                        elif q == Q - 1 and j == STEPS - 1:
                            sp.dma_start(win[:, :, q, WR - 2:WR, :], zeros).then_inc(win_loaded, 16)

                def send_acc(n, j):
                    s = STEPS * n + j
                    at_least(sp, x2_stored, 16 * Q * s)
                    sp.wait_ge(vadd_done, (SHIFTS) * (s + 1))
                    sp.wait_ge(padd_done, SHIFTS * (s + 1))
                    sp.wait_ge(add_out, s + 1)
                    for q in range(Q):
                        for h in range(CH):
                            g0 = G * q + h * (G // CH)
                            sp.dma_start(acc_t[:, h, q * TOK:(q + 1) * TOK], acc[g0:g0 + G // CH, :, :])\
                                .then_inc(acc_sent, 16)
                    for q in range(Q):
                        r0 = QR * q + SR * j
                        sp.dma_start(xres[:, :, q, :].rearrange("p h (r w) -> p h r w", w=W),
                                     image(x_v, n)[:, :, r0:r0 + SR, :]).then_inc(xres_loaded, 16)

                def store_x2(n, j):
                    s = STEPS * n + j
                    sp.wait_ge(stats2, 4 * (s + 1))
                    for q in range(Q):
                        r0 = QR * q + SR * j
                        sp.dma_start(image(x2_v, n)[:, :, r0:r0 + SR, :],
                                     xres[:, :, q, :].rearrange("p h (r w) -> p h r w", w=W))\
                            .then_inc(x2_stored, 16)

                load_window(0, 0)
                load_window(0, 1)

                def step(n, j, first, last):
                    if not first:
                        send_acc(*previous(n, j))
                    if not last and not (isinstance(n, int) and n == NI - 1 and j >= STEPS - 2):
                        n2, j2 = following(*following(n, j))
                        load_window(n2, j2)
                    if not first:
                        store_x2(*previous(n, j))

                steps_of_images(sp, step, None)
                send_acc(NI - 1, STEPS - 1)
                store_x2(NI - 1, STEPS - 1)
                sp.wait_ge(x2_stored, 16 * Q * STEPS * NI)

            def loads_before(n, j):
                return n * (STEPS * Q + 2) + j * Q + (1 if j > 0 else 0)

            @block.scalar
            def _(act):
                act.wait_ge(weights_loaded, WL)
                nc.scalar.mul(nomb[:, :], omb[:, :], -1.0).then_inc(abs_done, 1)
                act.wait_ge(abs_done, 1)
                act.wait_ge(val_zero, 1)

                def normalise(n, j):
                    n_loads = Q + (1 if j in (0, STEPS - 1) else 0)
                    nc.scalar.activation(gn[:, j % 2, :, :], tables[:, 0:2, bass.ds(n * CH, CH)], ACT.Copy)\
                        .then_inc(gn_kept, 1)
                    act.wait_ge(gn_kept, STEPS * n + j + 1)
                    act.wait_ge(win_loaded, 16 * (loads_before(n, j) + n_loads))
                    for h in range(CH):
                        scale, shift = gn[:, j % 2, 0, h:h + 1], gn[:, j % 2, 1, h:h + 1]
                        parts = [(0, Q, 0, WR)]
                        if j == 0:
                            parts = [(0, 1, 2, WR), (1, Q, 0, WR)]
                        elif j == STEPS - 1:
                            parts = [(0, Q - 1, 0, WR), (Q - 1, Q, 0, WR - 2)]
                        for q0, q1, r0, r1 in parts:
                            v = win[:, h, q0:q1, r0:r1, :]
                            last = nc.scalar.activation(v, v, ACT.Identity, bias=shift, scale=scale)
                    last.then_inc(win_normed, 1)

                def background(n, j):
                    unit = bg_before(n, j)
                    par = 0
                    for u in range(DW_UNITS):
                        h, qp = u // 2, u % 2
                        act.wait_ge(bg_full, unit + 1)
                        nc.scalar.activation(xdw[:, h, 2 * qp:2 * qp + 2, :], ps_bg[:, par, :], ACT.Identity,
                                             bias=dwb[:, h:h + 1]).then_inc(bg_free, 1)
                        unit, par = unit + 1, 1 - par
                    s = STEPS * n + j
                    at_least(act, vadd_done, SHIFTS * (s - 2)) if not isinstance(s, int) or s > 2 else None
                    at_least(act, padd_done, SHIFTS * (s - 2)) if not isinstance(s, int) or s > 2 else None
                    for g in row_groups(j):
                        for cp in range(V_UNITS):
                            act.wait_ge(bg_full, unit + 1)
                            for c in (2 * cp, 2 * cp + 1):
                                src = ps_bg[:, par, (c % 2) * TOK:(c % 2 + 1) * TOK].rearrange("p (r w) -> p r w", w=W)
                                parts = [(0, P, 0, SR)]
                                if g == 0:
                                    parts = [(0, G, 2, SR), (G, 2 * G, 0, SR), (2 * G, P, 0, SR)]
                                elif g == STEPS:
                                    parts = [(0, 2 * G, 0, SR), (2 * G, 3 * G, 0, SR), (3 * G, P, 0, 2)]
                                for p0, p1, r0, r1 in parts:
                                    last = nc.scalar.activation(
                                        val[p0:p1, c, SR * g + r0:SR * g + r1, 2:2 + W], src[p0:p1, r0:r1, :],
                                        ACT.Identity, bias=vpb[p0:p1, c:c + 1])
                            last.then_inc(bg_free, 1)
                            unit, par = unit + 1, 1 - par

                def hats(n, j, k):
                    t = (STEPS * n + j) * TAPS + k
                    par = (j + k) % 2
                    act.wait_ge(om_full, t + 1)
                    at_least(act, prod_done, t - 1)
                    nc.scalar.activation(msk[:, par, :], ps_m[:, 0, :], ACT.Identity,
                                         bias=omb[:, 18 + k:19 + k]).then_inc(msk_free, 1)
                    for a in range(2):
                        d, b, nb = ps_xy[:, par, a, :], omb[:, 2 * k + a:2 * k + a + 1], nomb[:, 2 * k + a:2 * k + a + 1]
                        nc.scalar.activation(hat[:, par, a, 1, :], d, ACT.Abs, bias=b).then_inc(abs_done, 1)
                    for a in range(2):
                        d, b, nb = ps_xy[:, par, a, :], omb[:, 2 * k + a:2 * k + a + 1], nomb[:, 2 * k + a:2 * k + a + 1]
                        nc.scalar.activation(hat[:, par, a, 0, :], d, ACT.Relu, bias=nb, scale=-1.0)
                        last = nc.scalar.activation(hat[:, par, a, 2, :], d, ACT.Relu, bias=b)
                    last.then_inc(om_free, 1)
                    act.wait_ge(abs_done, 1 + 2 * (t + 1))
                    if k == 0:
                        at_least(act, over_done, STEPS * n + j - 1)
                    nc.scalar.activation(over[:, :, :], hat[:, par, :, 1, :], ACT.Relu, bias=consts["minus1"][:, 0:1],
                                         accum_out=over_sum[:, j % 2, k:k + 1]).then_inc(w0_done, 1)
                    act.wait_ge(w0_done, t + 1)
                    nc.scalar.activation(hat[:, par, :, 1, :], hat[:, par, :, 1, :], ACT.Copy, bias=1.0,
                                         scale=-1.0).then_inc(hat_full, 1)

                def summed(n, j):
                    s = STEPS * n + j
                    act.wait_ge(add_done, SHIFTS * (s + 1))
                    at_least(act, acc_sent, 16 * CH * Q * s)
                    nc.scalar.activation(acc[:, 0:C_PE, :], ps_add[:, :, :], ACT.Copy).then_inc(add_out, 1)

                normalise(0, 0)
                background(0, 0)
                hats(0, 0, 0)
                hats(0, 0, 1)

                def step(n, j, first, last):
                    for k in range(2, TAPS):
                        hats(n, j, k)
                    if not last:
                        n1, j1 = following(n, j)
                        normalise(n1, j1)
                        background(n1, j1)
                        hats(n1, j1, 0)
                        hats(n1, j1, 1)
                    summed(n, j)

                steps_of_images(act, step, None)

            @block.tensor
            def _(pe):
                pe.wait_ge(weights_loaded, WL)
                pe.wait_ge(diag_made, CH * TAPS)

                def depthwise(n, j, u, part):
                    h, qp = u // 2, u % 2
                    bank = u % 2
                    out = ps_bg[:, bank, :].rearrange("p (q r w) -> p q r w", q=2, w=W)
                    order = [4, 0, 1, 2, 3, 5, 6, 7, 8]
                    if part == 0:
                        if u == 0:
                            pe.wait_ge(win_normed, STEPS * n + j + 1)
                        at_least(pe, bg_free, bg_before(n, j) + u - 1)
                    for i in range(3 * part, 3 * part + 3):
                        ky, kx = order[i] // 3, order[i] % 3
                        r0 = 1 + ky
                        o0, o1 = max(0, 1 - kx), W - max(0, kx - 1)
                        src = win[:, h, 2 * qp:2 * qp + 2, r0:r0 + SR, o0 + kx - 1:o1 + kx - 1]
                        mm = nc.tensor.matmul(out[:, :, :, o0:o1], diag[:, h, order[i], :], src,
                                              start=i == 0, stop=i == TAPS - 1)
                    if part == 2:
                        mm.then_inc(bg_full, 1)

                def values(n, j, gi, cp, ci):
                    g = row_groups(j)[gi]
                    u = DW_UNITS + gi * V_UNITS + cp
                    bank, c = u % 2, 2 * cp + ci
                    r0 = 0 if g == 0 else SR
                    if ci == 0:
                        at_least(pe, bg_free, bg_before(n, j) + u - 1)
                    for h in range(CH):
                        for q in range(Q):
                            mm = nc.tensor.matmul(ps_bg[G * q:G * q + G, bank, ci * TOK:(ci + 1) * TOK],
                                                  vpw[:, h, c, :], win[:, h, q, r0:r0 + SR, :],
                                                  start=h == 0, stop=h == CH - 1)
                    if ci == 1:
                        mm.then_inc(bg_full, 1)

                def offsets(n, j, k, part=None):
                    t = (STEPS * n + j) * TAPS + k
                    par = (j + k) % 2
                    for i in range(3) if part is None else [part]:
                        if i == 0:
                            if k == 0:
                                pe.wait_ge(bg_free, bg_before(n, j) + DW_UNITS)
                            at_least(pe, om_free, t - 1)
                        comp = (2 * k, 2 * k + 1, 18 + k)[i]
                        dst = (ps_xy[:, par, 0, :], ps_xy[:, par, 1, :], ps_m[:, 0, :])[i]
                        if i == 2:
                            at_least(pe, msk_free, t)
                        for h in range(CH):
                            for q in range(Q):
                                mm = nc.tensor.matmul(dst[G * q:G * q + G, :], omw[:, h, comp, :], xdw[:, h, q, :],
                                                      start=h == 0, stop=h == CH - 1)
                    if part in (None, 2):
                        mm.then_inc(om_full, 1)

                def project(n, j, u):
                    s = STEPS * n + j
                    oh, tb = u // 2, u % 2
                    if u == 0:
                        pe.wait_ge(acc_sent, 16 * CH * Q * (s + 1))
                    at_least(pe, pj_added, 4 * s + u - 1)
                    for h in range(CH):
                        mm = nc.tensor.matmul(ps_pj[:, u % 2, :], opw[:, h, P * oh:P * oh + P],
                                              acc_t[:, h, 512 * tb:512 * tb + 512], start=h == 0, stop=h == CH - 1)
                    mm.then_inc(pj_full, 1)

                def background(n, j):
                    out = [(depthwise, (n, j, u, part)) for u in range(DW_UNITS) for part in range(3)]
                    out += [(values, (n, j, gi, cp, ci)) for gi in range(len(row_groups(j)))
                            for cp in range(V_UNITS) for ci in range(2)]
                    out += [(offsets, (n, j, k, part)) for k in range(2) for part in range(3)]
                    return out

                def step(n, j, first, last):
                    s = STEPS * n + j
                    for k in range(2, TAPS):
                        offsets(n, j, k)
                    todo = [] if last else background(*following(n, j))
                    done = 0
                    for uv in range(SHIFTS):
                        if not first and uv in (2, 7, 12, 17):
                            project(*previous(n, j), (uv - 2) // 5)
                        upto = len(todo) * (uv + 1) // (SHIFTS - 1)
                        for f, args in todo[done:upto]:
                            f(*args)
                        done = max(done, upto)
                        pe.wait_ge(pv_full, SHIFTS * s + uv + 1)
                        if uv == 0:
                            at_least(pe, add_out, s)
                        nc.tensor.matmul(ps_add[:, :, :], consts["ident"][:, :], pv[:, uv % PBUF, 0:C_PE, :],
                                         start=uv == 0, stop=uv == SHIFTS - 1).then_inc(add_done, 1)

                for f, args in background(0, 0):
                    f(*args)
                steps_of_images(pe, step, None)
                for u in range(4):
                    project(NI - 1, STEPS - 1, u)

            @block.gpsimd
            def _(pool):
                nc.gpsimd.memset(val[:, :, :, :], 0.0).then_inc(val_zero, 1)

                def step(n, j, first, last):
                    s = STEPS * n + j
                    pool.wait_ge(wadd_done, (TAPS - 1) * (s + 1))
                    pool.wait_ge(bg_free, bg_before(*following(n, j)))
                    at_least(pool, acc_sent, 16 * CH * Q * s)
                    for uv in range(SHIFTS):
                        u, v = uv // D5, uv % D5
                        v_in = val[:, C_V:GC, SR * j + u:SR * j + u + SR, v:v + W]
                        w_in = wsum[:, j % 2, u, v, :].rearrange("p (r w) -> p r w", w=W).unsqueeze(1)\
                            .to_broadcast([P, C_POOL, SR, W])
                        dst = acc[:, C_V:GC, :] if uv == 0 else pp[:, :, :]
                        ins = nc.gpsimd.tensor_tensor(dst.rearrange("p c (r w) -> p c r w", w=W), v_in, w_in, ALU.mult)
                        if uv == 0:
                            ins.then_inc(padd_done, 1)
                            pool.wait_ge(padd_done, SHIFTS * s + 1)
                        else:
                            ins.then_inc(pmul_done, 1)
                            pool.wait_ge(pmul_done, (SHIFTS - 1) * s + uv)
                            nc.gpsimd.tensor_tensor(acc[:, C_V:GC, :], acc[:, C_V:GC, :], pp[:, :, :], ALU.add)\
                                .then_inc(padd_done, 1)
                            pool.wait_ge(padd_done, SHIFTS * s + uv + 1)

                steps_of_images(pool, step, None)

            @block.vector
            def _(dve):
                dve.wait_ge(weights_loaded, WL)
                for h in range(CH):
                    for k in range(TAPS):
                        nc.vector.tensor_scalar(diag[:, h, k, :], consts["ident"][:, :], dww[:, h, k:k + 1], None,
                                                ALU.mult).then_inc(diag_made, 1)
                nc.vector.memset(over_max[:, :], 0.0).then_inc(diag_made, 1)
                dve.wait_ge(diag_made, CH * TAPS + 1)

                def weights(n, j):
                    s = STEPS * n + j
                    ws = wsum[:, j % 2, :, :, :]
                    at_least(dve, padd_done, SHIFTS * (s - 1)) if not isinstance(s, int) or s > 1 else None

                    def mask_rows(k):
                        t, par = TAPS * s + k, (j + k) % 2
                        dve.wait_ge(hat_full, t + 1)
                        nc.vector.tensor_tensor(mwy[:, :, :], hat[:, par, 1, :, :],
                                                msk[:, par, :].unsqueeze(1).to_broadcast([P, 3, TOK]), ALU.mult)\
                            .then_inc(mwy_done, 1)

                    def product(dst, k, rect):
                        a, b, c, d = rect
                        par = (j + k) % 2
                        shape = [P, b - a, d - c, TOK]
                        return nc.vector.tensor_tensor(
                            dst, hat[:, par, 0, c:d, :].unsqueeze(1).to_broadcast(shape),
                            mwy[:, a:b, :].unsqueeze(2).to_broadcast(shape), ALU.mult)

                    mask_rows(0)
                    for k in range(TAPS):
                        t = TAPS * s + k
                        ky, kx = k // 3, k % 3
                        new, old = tap_rects(ky, kx)
                        dve.wait_ge(mwy_done, t + 1)
                        if k > 1:
                            dve.wait_ge(wadd_done, (TAPS - 1) * s + k - 1)
                        for a, b, c, d in old:
                            product(prod[:, a:b, c:d, :], k, (a, b, c, d))
                        for a, b, c, d in new:
                            ins = product(ws[:, ky + a:ky + b, kx + c:kx + d, :], k, (a, b, c, d))
                        ins.then_inc(prod_done, 1)
                        dve.wait_ge(prod_done, t + 1)
                        if k + 1 < TAPS:
                            mask_rows(k + 1)
                        for a, b, c, d in old:
                            w = ws[:, ky + a:ky + b, kx + c:kx + d, :]
                            ins = nc.vector.tensor_tensor(w, w, prod[:, a:b, c:d, :], ALU.add)
                        if k > 0:
                            ins.then_inc(wadd_done, 1)
                    dve.wait_ge(wadd_done, (TAPS - 1) * (s + 1))

                def sample(n, j, first):
                    s = STEPS * n + j
                    dve.wait_ge(bg_free, bg_before(*following(n, j)))
                    at_least(dve, acc_sent, 16 * CH * Q * s)

                    def multiply(uv):
                        u, v = uv // D5, uv % D5
                        at_least(dve, add_done, SHIFTS * s + uv - PBUF + 1) if not isinstance(s, int) or s > 0 or uv >= PBUF else None
                        w_in = wsum[:, j % 2, u, v, :].rearrange("p (r w) -> p r w", w=W).unsqueeze(1)\
                            .to_broadcast([P, C_V, SR, W])
                        nc.vector.tensor_tensor(pv[:, uv % PBUF, :, :].rearrange("p c (r w) -> p c r w", w=W),
                                                val[:, 0:C_V, SR * j + u:SR * j + u + SR, v:v + W], w_in, ALU.mult)\
                            .then_inc(pv_full, 1)

                    def add(uv):
                        a = acc[:, C_PE:C_V, :]
                        dve.wait_ge(pv_full, SHIFTS * s + uv + 1)
                        p = pv[:, uv % PBUF, C_PE:C_V, :]
                        if uv == 0:
                            ins = nc.vector.tensor_copy(a, p)
                        else:
                            dve.wait_ge(vadd_done, SHIFTS * s + uv)
                            ins = nc.vector.tensor_tensor(a, a, p, ALU.add)
                        ins.then_inc(vadd_done, 1)

                    multiply(0)
                    for uv in range(SHIFTS):
                        if uv + 1 < SHIFTS:
                            multiply(uv + 1)
                        add(uv)
                        if not first and uv in (5, 10, 15, 20):
                            residual(*previous(n, j), uv // 5 - 1)
                    if j == 1 and not (isinstance(n, int) and n == 0):
                        aggregate(n - 1)
                    if not first:
                        statistics(*previous(n, j))

                def residual(n, j, u):
                    s = STEPS * n + j
                    oh, tb = u // 2, u % 2
                    if u == 0:
                        dve.wait_ge(xres_loaded, 16 * Q * (s + 1))
                    dve.wait_ge(pj_full, 4 * s + u + 1)
                    v = xres[:, oh, 2 * tb:2 * tb + 2, :].rearrange("p q t -> p (q t)")
                    nc.vector.tensor_tensor(v, ps_pj[:, u % 2, :], v, ALU.add).then_inc(pj_added, 1)

                def statistics(n, j):
                    s = STEPS * n + j
                    dve.wait_ge(pj_added, 4 * (s + 1))
                    for u in range(4):
                        oh, tb = u // 2, u % 2
                        nc.vector.bn_stats(bs2[:, oh, 2 * j + tb, :], xres[:, oh, 2 * tb:2 * tb + 2, :].rearrange("p q t -> p (q t)"))\
                            .then_inc(stats2, 1)

                def aggregate(n):
                    for h in range(CH):
                        nc.vector.bn_aggr(mv_now[:, h, :], bs2[:, h, :, :]).then_inc(aggr2, 1)
                    dve.wait_ge(aggr2, CH * (n + 1))
                    nc.vector.tensor_scalar(mv2[:, bass.ds(n, 1), :, :].rearrange("p n h s -> p (n h s)"),
                                            mv_now[:, :, :].rearrange("p h s -> p (h s)"), 1.0, None,
                                            ALU.mult).then_inc(mv_kept, 1)

                def reach_of(n, j):
                    s = STEPS * n + j
                    nc.vector.tensor_reduce(consts["spare"][:, j % 2:j % 2 + 1], over_sum[:, j % 2, :], AX_X, ALU.max)\
                        .then_inc(over_done, 1)
                    dve.wait_ge(over_done, s + 1)
                    nc.vector.tensor_tensor(over_max[:, :], over_max[:, :], consts["spare"][:, j % 2:j % 2 + 1], ALU.max)

                def step(n, j, first, last):
                    weights(n, j)
                    reach_of(n, j)
                    sample(n, j, first)

                steps_of_images(dve, step, None)
                for u in range(4):
                    residual(NI - 1, STEPS - 1, u)
                statistics(NI - 1, STEPS - 1)
                dve.wait_ge(stats2, 4 * STEPS * NI)
                dve.wait_ge(mv_kept, NI - 1)
                aggregate(NI - 1)
                dve.wait_ge(mv_kept, NI)
                nc.vector.tensor_copy(reach[:, :], over_max[:, :]).then_inc(over_done, 1)
                dve.wait_ge(over_done, STEPS * NI + 1)


def layer0_any_offset(nc, x, w_dram, x2, consts, tables, mv2, reach, NI):
    R = FARTHEST
    PADH = H + 2 * R
    vpad = nc.dram_tensor("vpad", (C, PADH, PADH), F32, kind="Internal").ap()
    CT = 512
    with ExitStack() as ctx:
        sb = lambda name, shape, dt=F32: ctx.enter_context(nc.sbuf_tensor(name, shape, dt))
        sem = lambda name: ctx.enter_context(nc.semaphore(name))
        xi = sb("g_x", [P, CH, HW])
        xpad = sb("g_xpad", [P, CH, H + 2, W + 2])
        xdw = sb("g_xdw", [P, CH, HW])
        xdw_step = xi[:, :, 0:Q * TOK].rearrange("p h (q t) -> p h q t", q=Q)
        prj = xi[:, :, Q * TOK:2 * Q * TOK].rearrange("p h (q t) -> p h q t", q=Q)
        off = sb("g_off", [P, 3, TAPS, TOK])
        wx = sb("g_wx", [P, TAPS, TOK])
        wy = sb("g_wy", [P, TAPS, TOK])
        rows = sb("g_rows", [P, GC, SR, PADH])
        acc = sb("g_acc", [P, GC, TOK])
        tmp = sb("g_tmp", [P, GC, TOK])
        acc_t = tmp[:, :, :].rearrange("p c t -> p (c t)").rearrange("p (h t) -> p h t", h=CH)
        xres = acc[:, :, :].rearrange("p c t -> p (c t)").rearrange("p (h q t) -> p h q t", h=CH, q=Q)
        w = sb("g_w", [P, TOK])
        at_y = sb("g_at_y", [P, 1])
        at_x = sb("g_at_x", [P, 1])
        gn = sb("g_gn", [P, 2, CH])
        bs = sb("g_bs", [P, CH, HW // CT, 6])
        mv_now = sb("g_mv", [P, CH, 2])
        omw = sb("g_omw", [P, CH, 27, G])
        vpw = sb("g_vpw", [P, CH, C])
        opw = sb("g_opw", [P, CH, C])
        dww = sb("g_dww", [P, CH, TAPS])
        dwb = sb("g_dwb", [P, CH])
        omb = sb("g_omb", [P, 27])
        vpb = sb("g_vpb", [P, CH])
        ones = sb("g_ones", [P, P])
        flag = sb("g_flag", [P, 1], mybir.dt.int32)
        ps = ctx.enter_context(nc.psum_tensor("g_ps", [P, 8, CT], F32))

        flag_summed, flag_made, loaded = sem("flag_summed"), sem("flag_made"), sem("g_loaded")
        with nc.Block() as block:
            @block.sync
            def _(sp):
                sp.dma_start(ones[:, :], w_dram["mean256"]).then_inc(loaded, 16)
                sp.wait_ge(loaded, 16)

            @block.tensor
            def _(pe):
                pe.wait_ge(loaded, 16)
                nc.tensor.matmul(ps[:, 0, 0:1], ones[:, :], reach[:, :], start=True, stop=True).then_inc(flag_summed, 1)

            @block.vector
            def _(dve):
                dve.wait_ge(flag_summed, 1)
                nc.vector.tensor_scalar(flag[:, :], ps[:, 0, 0:1], 0.0, None, ALU.is_gt).then_inc(flag_made, 1)
                dve.wait_ge(flag_made, 1)

        s_zero, s_zeroed, s_weights = sem("g_zero"), sem("g_zeroed"), sem("g_weights")
        x_in, x_normed_v, x_normed_d, v_bank, v_read = sem("g_x_in"), sem("g_nv"), sem("g_nd"), sem("g_vb"), sem("g_vr")
        v_ready, v_kept, xi_free = sem("g_v_ready"), sem("g_v_kept"), sem("g_xi_free")
        dw_step, om_bank, om_read = sem("g_dw_step"), sem("g_om_bank"), sem("g_om_read")
        rows_in, rows_used, acc_ready, acc_in = sem("g_rows_in"), sem("g_rows_used"), sem("g_acc_ready"), sem("g_acc_in")
        xres_in, pj_bank, pj_read = sem("g_xres_in"), sem("g_pj_bank"), sem("g_pj_read")
        x2_ready, x2_kept, x2_in, x2_used = sem("g_x2_ready"), sem("g_x2_kept"), sem("g_x2_in"), sem("g_x2_used")
        chain_a, pj_out, x_free = sem("g_chain_a"), sem("g_pj_out"), sem("g_x_free")
        gn_kept, chain, kept_dma = sem("g_gn_kept"), sem("g_chain"), sem("g_kept_dma")

        def take(eng, s, value):
            eng.wait_ge(s, value)
            eng.sem_clear(s)

        x_v = x.rearrange("n (h p) t -> n p h t", p=P)
        x2_v = x2.rearrange("n (h p) t -> n p h t", p=P)
        vpad_c = vpad.rearrange("(h p) y x -> p h y x", p=P)
        vpad_g = vpad.rearrange("(g c) y x -> g c y x", c=GC)
        of_image = lambda v, n: v[bass.ds(n, 1)].rearrange("n p h t -> p (n h) t")

        with nc.Block() as block:
            @block.sync
            def _(sp):
                with sp.If(sp.value_load(flag[0:1, 0:1], min_val=0, max_val=1) > 0):
                    for dst, name in ((dww, "dww"), (dwb, "dwb"), (omw, "omw"), (omb, "omb"), (vpw, "vpw_c"),
                                      (vpb, "vpb_c"), (opw, "opw")):
                        sp.dma_start(dst[:], w_dram[name]).then_inc(s_weights, 16)
                    sp.wait_ge(s_weights, 16 * 7)
                    take(sp, s_zero, 1)
                    zero = rows[:, :, :, :].rearrange("p c r x -> p (c r) x")
                    for h in range(CH):
                        for y in range(0, PADH, GC * SR):
                            k = min(GC * SR, PADH - y)
                            sp.dma_start(vpad_c[:, h, y:y + k, :], zero[:, 0:k, :]).then_inc(s_zeroed, 16)
                    sp.wait_ge(s_zeroed, 16 * CH * -(-PADH // (GC * SR)))
                    with sp.Fori(0, NI) as n:
                        sp.dma_start(xi[:, :, :], of_image(x_v, n)).then_inc(x_in, 16)
                        take(sp, v_ready, 1)
                        for h in range(CH):
                            sp.dma_start(vpad_c[:, h, R:R + H, R:R + W],
                                         xi[:, h, :].rearrange("p (r w) -> p r w", w=W)).then_inc(kept_dma, 16)
                        take(sp, kept_dma, 16 * CH)
                        sp.nop().then_inc(v_kept, 1)
                        with sp.Fori(0, STEPS) as j:
                            with sp.Fori(0, 2 * R + 1) as u:
                                take(sp, rows_used, 1)
                                for q in range(Q):
                                    sp.dma_start(rows[G * q:G * q + G, :, :, :],
                                                 vpad_g[:, :, bass.ds(j * SR + u + QR * q, SR), :]).then_inc(rows_in, 16)
                            take(sp, acc_ready, 1)
                            for q in range(Q):
                                for h in range(CH):
                                    g0 = G * q + h * (G // CH)
                                    sp.dma_start(acc_t[:, h, q * TOK:(q + 1) * TOK], acc[g0:g0 + G // CH, :, :])\
                                        .then_inc(kept_dma, 16)
                            take(sp, kept_dma, 16 * CH * Q)
                            sp.nop().then_inc(acc_in, 1)
                            for q in range(Q):
                                sp.dma_start(xres[:, :, q, :],
                                             of_image(x_v, n)[:, :, bass.ds(j * TOK + QR * W * q, TOK)]).then_inc(xres_in, 16)
                            take(sp, x2_ready, 1)
                            for q in range(Q):
                                sp.dma_start(of_image(x2_v, n)[:, :, bass.ds(j * TOK + QR * W * q, TOK)],
                                             xres[:, :, q, :]).then_inc(kept_dma, 16)
                            take(sp, kept_dma, 16 * Q)
                            sp.nop().then_inc(x2_kept, 1)
                        sp.dma_start(xi[:, :, :], of_image(x2_v, n)).then_inc(x2_in, 16)
                        take(sp, x2_used, 1)

            @block.scalar
            def _(act):
                with act.If(act.value_load(flag[0:1, 0:1], min_val=0, max_val=1) > 0):
                    act.wait_ge(s_weights, 16 * 7)
                    take(act, x_free, 1)
                    with act.Fori(0, NI) as n:
                        nc.scalar.activation(gn[:, :, :], tables[:, 0:2, bass.ds(n * CH, CH)], ACT.Copy).then_inc(gn_kept, 1)
                        take(act, gn_kept, 1)
                        take(act, x_in, 16)
                        for h in range(CH):
                            last = nc.scalar.activation(xpad[:, h, 1:1 + H, 1:1 + W],
                                                        xi[:, h, :].rearrange("p (r w) -> p r w", w=W), ACT.Identity,
                                                        bias=gn[:, 1, h:h + 1], scale=gn[:, 0, h:h + 1])
                            last.then_inc(x_normed_v, 1)
                        take(act, x_normed_v, CH)
                        nc.scalar.nop().then_inc(x_normed_d, 1)
                        nc.scalar.nop().then_inc(v_read, 1)
                        for u in range(CH * HW // CT):
                            h, t = u % CH, u // CH
                            take(act, v_bank, 1)
                            nc.scalar.activation(xi[:, h, CT * t:CT * t + CT], ps[:, 0, :], ACT.Identity,
                                                 bias=vpb[:, h:h + 1]).then_inc(chain_a, 1)
                            take(act, chain_a, 1)
                            nc.scalar.nop().then_inc(v_read if u + 1 < CH * HW // CT else v_ready, 1)
                        with act.Fori(0, STEPS) as j:
                            for u in range(4):
                                oh, tb = u // 2, u % 2
                                take(act, pj_bank, 1)
                                nc.scalar.activation(prj[:, oh, 2 * tb:2 * tb + 2, :], ps[:, 0, :].rearrange(
                                    "p (q t) -> p q t", q=2), ACT.Copy).then_inc(chain_a, 1)
                                take(act, chain_a, 1)
                                nc.scalar.nop().then_inc(pj_read if u < 3 else pj_out, 1)

            @block.tensor
            def _(pe):
                with pe.If(pe.value_load(flag[0:1, 0:1], min_val=0, max_val=1) > 0):
                    pe.wait_ge(s_weights, 16 * 7)
                    with pe.Fori(0, NI) as n:
                        for u in range(CH * HW // CT):
                            oh, t = u % CH, u // CH
                            take(pe, v_read, 1)
                            for h in range(CH):
                                mm = nc.tensor.matmul(ps[:, 0, :].rearrange("p (r w) -> p r w", w=W),
                                                      vpw[:, h, P * oh:P * oh + P],
                                                      xpad[:, h, 8 * t + 1:8 * t + 9, 1:1 + W],
                                                      start=h == 0, stop=h == CH - 1)
                            mm.then_inc(v_bank, 1)
                        with pe.Fori(0, STEPS) as j:
                            for u in range(27):
                                take(pe, dw_step if u == 0 else om_read, 1)
                                for h in range(CH):
                                    for q in range(Q):
                                        mm = nc.tensor.matmul(ps[G * q:G * q + G, 1, 0:TOK], omw[:, h, u, :],
                                                              xdw_step[:, h, q, :], start=h == 0, stop=h == CH - 1)
                                mm.then_inc(om_bank, 1)
                            for u in range(4):
                                oh, tb = u // 2, u % 2
                                take(pe, acc_in if u == 0 else pj_read, 1)
                                for h in range(CH):
                                    mm = nc.tensor.matmul(ps[:, 0, :], opw[:, h, P * oh:P * oh + P],
                                                          acc_t[:, h, CT * tb:CT * tb + CT],
                                                          start=h == 0, stop=h == CH - 1)
                                mm.then_inc(pj_bank, 1)

            @block.vector
            def _(dve):
                def link(ins):
                    ins.then_inc(chain, 1)
                    take(dve, chain, 1)

                with dve.If(dve.value_load(flag[0:1, 0:1], min_val=0, max_val=1) > 0):
                    link(nc.vector.memset(rows[:, :, :, :], 0.0))
                    nc.vector.nop().then_inc(s_zero, 1)
                    link(nc.vector.memset(xpad[:, :, :, :], 0.0))
                    dve.wait_ge(s_weights, 16 * 7)
                    dve.wait_ge(s_zeroed, 16 * CH * -(-PADH // (GC * SR)))
                    nc.vector.nop().then_inc(x_free, 1)
                    with dve.Fori(0, NI) as n:
                        take(dve, x_normed_d, 1)
                        for h in range(CH):
                            dst = xdw[:, h, :].rearrange("p (r w) -> p r w", w=W)
                            for k in range(TAPS):
                                src = xpad[:, h, k // 3:k // 3 + H, k % 3:k % 3 + W]
                                if k == 0:
                                    link(nc.vector.tensor_scalar(dst, src, dww[:, h, 0:1], dwb[:, h:h + 1],
                                                                 ALU.mult, ALU.add))
                                else:
                                    link(nc.vector.scalar_tensor_tensor(out=dst, in0=src, scalar=dww[:, h, k:k + 1],
                                                                        in1=dst, op0=ALU.mult, op1=ALU.add))
                        take(dve, v_kept, 1)
                        with dve.Fori(0, STEPS) as j:
                            for h in range(CH):
                                for q in range(Q):
                                    link(nc.vector.tensor_copy(xdw_step[:, h, q, :],
                                                               xdw[:, h, bass.ds(j * TOK + QR * W * q, TOK)]))
                            nc.vector.nop().then_inc(dw_step, 1)
                            for u in range(27):
                                take(dve, om_bank, 1)
                                if u < 2 * TAPS:
                                    k, axis = u // 2, u % 2
                                    shift = float((k % 3, k // 3)[axis] - 1)
                                    link(nc.vector.tensor_scalar(off[:, axis, k, :], ps[:, 1, 0:TOK], omb[:, u:u + 1],
                                                                 shift, ALU.add, ALU.add))
                                else:
                                    link(nc.vector.tensor_scalar(off[:, 2, u - 2 * TAPS, :], ps[:, 1, 0:TOK],
                                                                 omb[:, u:u + 1], None, ALU.add))
                                if u < 26:
                                    nc.vector.nop().then_inc(om_read, 1)
                            link(nc.vector.memset(acc[:, :, :], 0.0))
                            link(nc.vector.memset(at_y[:, :], float(-R)))
                            with dve.Fori(0, 2 * R + 1) as u:
                                nc.vector.nop().then_inc(rows_used, 1)
                                link(nc.vector.tensor_scalar(wy[:, :, :], off[:, 1, :, :], at_y[:, 0:1], None, ALU.subtract))
                                link(nc.vector.scalar_tensor_tensor(out=wy[:, :, :], in0=wy[:, :, :], scalar=-1.0,
                                                                    in1=wy[:, :, :], op0=ALU.mult, op1=ALU.max))
                                link(nc.vector.tensor_scalar(wy[:, :, :], wy[:, :, :], 1.0, -1.0, ALU.min, ALU.mult))
                                link(nc.vector.scalar_tensor_tensor(out=wy[:, :, :], in0=wy[:, :, :], scalar=1.0,
                                                                    in1=off[:, 2, :, :], op0=ALU.add, op1=ALU.mult))
                                link(nc.vector.tensor_scalar(at_y[:, :], at_y[:, :], 1.0, None, ALU.add))
                                link(nc.vector.memset(at_x[:, :], float(-R)))
                                take(dve, rows_in, 16 * Q)
                                with dve.Fori(0, 2 * R + 1) as v:
                                    link(nc.vector.tensor_scalar(wx[:, :, :], off[:, 0, :, :], at_x[:, 0:1], None, ALU.subtract))
                                    link(nc.vector.scalar_tensor_tensor(out=wx[:, :, :], in0=wx[:, :, :], scalar=-1.0,
                                                                        in1=wx[:, :, :], op0=ALU.mult, op1=ALU.max))
                                    link(nc.vector.tensor_scalar(wx[:, :, :], wx[:, :, :], 1.0, -1.0, ALU.min, ALU.mult))
                                    link(nc.vector.scalar_tensor_tensor(out=wx[:, :, :], in0=wx[:, :, :], scalar=1.0,
                                                                        in1=wy[:, :, :], op0=ALU.add, op1=ALU.mult))
                                    link(nc.vector.tensor_reduce(w[:, :], wx[:, :, :].rearrange("p k t -> p t k"),
                                                                 AX_X, ALU.add))
                                    link(nc.vector.tensor_tensor(
                                        tmp[:, :, :].rearrange("p c (r w) -> p c r w", w=W),
                                        rows[:, :, :, bass.ds(v, W)],
                                        w[:, :].rearrange("p (r w) -> p r w", w=W).unsqueeze(1)
                                        .to_broadcast([P, GC, SR, W]), ALU.mult))
                                    link(nc.vector.tensor_tensor(acc[:, :, :], acc[:, :, :], tmp[:, :, :], ALU.add))
                                    link(nc.vector.tensor_scalar(at_x[:, :], at_x[:, :], 1.0, None, ALU.add))
                            nc.vector.nop().then_inc(acc_ready, 1)
                            take(dve, pj_out, 1)
                            take(dve, xres_in, 16 * Q)
                            link(nc.vector.tensor_tensor(xres, xres, prj, ALU.add))
                            nc.vector.nop().then_inc(x2_ready, 1)
                            take(dve, x2_kept, 1)
                        take(dve, x2_in, 16)
                        for h in range(CH):
                            for i in range(HW // CT):
                                link(nc.vector.bn_stats(bs[:, h, i, :], xi[:, h, CT * i:CT * i + CT]))
                            link(nc.vector.bn_aggr(mv_now[:, h, :], bs[:, h, :, :]))
                        link(nc.vector.tensor_copy(mv2[:, bass.ds(n, 1), :, :].rearrange("p n h s -> p (n h s)"),
                                                   mv_now[:, :, :].rearrange("p h s -> p (h s)")))
                        nc.vector.nop().then_inc(x2_used, 1)


def layer1(nc, x2, w_dram, out, consts, tables, NI):
    CT = HW // 8
    CHUNKS = 8
    UNITS = CHUNKS * CH
    BANKS = 4
    PAD = H + 2
    with ExitStack() as ctx:
        sb = lambda name, shape, dt=F32: ctx.enter_context(nc.sbuf_tensor(name, shape, dt))
        sem = lambda name: ctx.enter_context(nc.semaphore(name))
        xb = sb("c_x", [P, 2, CH, HW])
        sgn = sb("c_sgn", [P, 2, CH, PAD, PAD], BF16)
        size = sb("c_size", [P, 2, CH, CT])
        beta = sb("c_beta", [P, PAD, PAD])
        hsum = sb("c_hsum", [P, PAD, W])
        box = sb("c_box", [P, 2, H, W])
        kern = sb("c_kern", [P, TAPS, C])
        ksgn = sb("c_ksgn", [P, CH, TAPS, C], BF16)
        res = sb("c_res", [P, BANKS, CT])
        mean256 = sb("c_mean", [P, P])
        bias = sb("c_bias", [P, CH])
        scale = sb("c_scale", [P, CH])
        gn = sb("c_gn", [P, 2, 2, CH])
        gn_kept = sem("c_gn_kept")
        ps_c = [ctx.enter_context(nc.psum_tensor(f"ps_c{i}", [P, 8, W], F32)) for i in range(BANKS)]
        ps_b = [ctx.enter_context(nc.psum_tensor(f"ps_b{i}", [P, 8, W], F32)) for i in range(2)]
        ps_alpha = [ctx.enter_context(nc.psum_tensor(f"ps_alpha{i}", [P, 512], F32)) for i in range(CH)]
        alpha_kept = sem("alpha_kept")

        consts_loaded, kern_loaded = sem("c_consts"), sem("kern_loaded")
        kern_signed, kern_sized, alpha_part = sem("kern_signed"), sem("kern_sized"), sem("alpha_part")
        scale_made, cleared, pool_cleared = sem("scale_made"), sem("cleared"), sem("pool_cleared")
        x_loaded = [sem(f"c_loaded{b}") for b in range(2)]
        signed, sized, beta_full, beta_out = sem("signed"), sem("sized"), sem("beta_full"), sem("beta_out")
        hsum_done, box_half, box_done = sem("hsum_done"), sem("box_half"), sem("box_done")
        conv_full, mult_done, affine_done, added = sem("conv_full"), sem("mult_done"), sem("affine_done"), sem("added")
        stored = sem("stored")
        QUARTERS = 4

        def images(eng, image):
            for b in range(2):
                image(b, b, False)
            if NI > 4:
                with eng.Fori(1, NI // 2 - 1) as m:
                    for b in range(2):
                        image(2 * m + b, b, False)
            for b in range(2):
                image(NI - 2 + b, b, b == 1)

        def of_image(v, n):
            return v[n] if isinstance(n, int) else v[bass.ds(n, 1)].rearrange("n p h t -> p (n h) t")

        x2_v = x2.rearrange("n (h p) t -> n p h t", p=P)
        out_v = out.rearrange("n (h p) t -> n p h t", p=P)

        def pair(n, b):
            return n // 2 if isinstance(n, int) else (n - b) // 2

        with nc.Block() as block:
            @block.sync
            def _(sp):
                sp.dma_start(mean256[:, :], w_dram["mean256"]).then_inc(consts_loaded, 16)
                sp.dma_start(bias[:, :], w_dram["bias"]).then_inc(consts_loaded, 16)
                for h in range(CH):
                    if h > 0:
                        sp.wait_ge(alpha_part, h)
                    sp.dma_start(kern[:, :, :], w_dram["kernel"][:, h]).then_inc(kern_loaded, 16)
                    if h == 0:
                        for b in range(2):
                            sp.dma_start(xb[:, b, :, :], x2_v[b]).then_inc(x_loaded[b], 16)

                def image(n, b, last):
                    for i in range(QUARTERS):
                        sp.wait_ge(added, UNITS * n + UNITS // QUARTERS * (i + 1))
                        at = slice(HW // QUARTERS * i, HW // QUARTERS * (i + 1))
                        sp.dma_start(of_image(out_v, n)[:, :, at], xb[:, b, :, at]).then_inc(stored, 16)
                    if isinstance(n, int) and n + 2 >= NI:
                        return
                    sp.wait_ge(stored, 16 * QUARTERS * (n + 1))
                    sp.dma_start(xb[:, b, :, :], of_image(x2_v, n + 2)).then_inc(x_loaded[b], 16)

                images(sp, image)
                sp.wait_ge(stored, 16 * QUARTERS * NI)

            @block.scalar
            def _(act):
                for h in range(CH):
                    act.wait_ge(kern_signed, h + 1)
                    nc.scalar.activation(kern[:, :, :], kern[:, :, :], ACT.Abs).then_inc(kern_sized, 1)
                act.wait_ge(scale_made, 1)
                act.wait_ge(cleared, 1)
                act.wait_ge(consts_loaded, 32)

                def sizes(n, b, t):
                    i = CHUNKS * n + t
                    if t == 0:
                        nc.scalar.activation(gn[:, b, :, :], tables[:, 0:2, bass.ds(n * CH, CH)], ACT.Copy)\
                            .then_inc(gn_kept, 1)
                        act.wait_ge(gn_kept, n + 1)
                        act.wait_ge(x_loaded[b], 16 * (pair_of[0] + 1))
                    at_least(act, beta_full, i - 1) if not isinstance(i, int) or i > 1 else None
                    for h in range(CH):
                        last = nc.scalar.activation(size[:, t % 2, h, :], xb[:, b, h, CT * t:CT * t + CT], ACT.Abs,
                                                    bias=gn[:, b, 1, h:h + 1], scale=gn[:, b, 0, h:h + 1])
                    last.then_inc(sized, 1)

                def keep_beta(n, t):
                    act.wait_ge(beta_full, CHUNKS * n + t + 1)
                    at_least(act, box_done, CHUNKS * n)
                    nc.scalar.activation(beta[:, 8 * t + 1:8 * t + 9, 1:1 + W], ps_b[t % 2][:, :, :], ACT.Copy)\
                        .then_inc(beta_out, 1)

                pair_of = [0]
                for t in range(CHUNKS):
                    sizes(0, 0, t)
                    if t > 0:
                        keep_beta(0, t - 1)
                keep_beta(0, CHUNKS - 1)

                def image(n, b, last):
                    pair_of[0] = pair(n, b) + b
                    for u in range(UNITS):
                        t = u - UNITS // 2
                        if t >= 0 and not last:
                            sizes(n + 1, 1 - b, t)
                        act.wait_ge(mult_done, UNITS * n + u + 1)
                        v = res[:, u % BANKS, :]
                        nc.scalar.activation(v, v, ACT.Identity, bias=bias[:, u % CH:u % CH + 1],
                                             scale=scale[:, u % CH:u % CH + 1]).then_inc(affine_done, 1)
                        if t >= 1 and not last:
                            keep_beta(n + 1, t - 1)
                    if not last:
                        keep_beta(n + 1, CHUNKS - 1)

                images(act, image)

            @block.tensor
            def _(pe):
                pe.wait_ge(consts_loaded, 32)
                for h in range(CH):
                    pe.wait_ge(kern_sized, h + 1)
                    for oh in range(CH):
                        for k in range(TAPS):
                            mm = nc.tensor.matmul(ps_alpha[h][:, oh:oh + 1], kern[:, k, P * oh:P * oh + P],
                                                  mean256[:, 0:1], start=k == 0, stop=k == TAPS - 1)
                    mm.then_inc(alpha_part, 1)
                pe.wait_ge(scale_made, 1)

                def mean_size(n, t):
                    i = CHUNKS * n + t
                    pe.wait_ge(sized, i + 1)
                    at_least(pe, beta_out, i - 1) if not isinstance(i, int) or i > 1 else None
                    for h in range(CH):
                        mm = nc.tensor.matmul(ps_b[t % 2][:, :, :], mean256[:, :], size[:, t % 2, h, :],
                                              start=h == 0, stop=h == CH - 1)
                    mm.then_inc(beta_full, 1)

                for t in range(CHUNKS):
                    mean_size(0, t)

                def image(n, b, last):
                    pe.wait_ge(signed, CH * (n + 1))
                    for u in range(UNITS):
                        t, oh = u // CH, u % CH
                        i = UNITS * n + u
                        at_least(pe, mult_done, i - BANKS + 1) if not isinstance(i, int) or i >= BANKS else None
                        for h in range(CH):
                            for k in range(TAPS):
                                ky, kx = k // 3, k % 3
                                mm = nc.tensor.matmul(
                                    ps_c[u % BANKS][:, :, :], ksgn[:, h, k, P * oh:P * oh + P],
                                    sgn[:, b, h, 8 * t + ky:8 * t + ky + 8, kx:kx + W],
                                    start=h == 0 and k == 0, stop=h == CH - 1 and k == TAPS - 1)
                        mm.then_inc(conv_full, 1)
                        if u >= UNITS // 2 and not last:
                            mean_size(n + 1, u - UNITS // 2)

                images(pe, image)

            @block.gpsimd
            def _(pool):
                nc.gpsimd.memset(hsum[:, :, :], 0.0).then_inc(pool_cleared, 1)
                pool.wait_ge(pool_cleared, 1)
                pool.wait_ge(cleared, 1)

                def across(n, t):
                    pool.wait_ge(beta_out, CHUNKS * n + t + 1)
                    at_least(pool, box_done, CHUNKS * n)
                    r = slice(8 * t + 1, 8 * t + 9)
                    nc.gpsimd.tensor_tensor(hsum[:, r, :], beta[:, r, 0:W], beta[:, r, 1:1 + W], ALU.add)\
                        .then_inc(hsum_done, 1)
                    pool.wait_ge(hsum_done, 2 * (CHUNKS * n + t) + 1)
                    nc.gpsimd.tensor_tensor(hsum[:, r, :], hsum[:, r, :], beta[:, r, 2:2 + W], ALU.add)\
                        .then_inc(hsum_done, 1)

                def down(n, b, t):
                    i = CHUNKS * n + t
                    pool.wait_ge(hsum_done, 2 * (CHUNKS * n + min(t + 2, CHUNKS)))
                    at_least(pool, mult_done, UNITS * (n - 1)) if not isinstance(n, int) or n > 1 else None
                    dst = box[:, b, 8 * t:8 * t + 8, :]
                    nc.gpsimd.tensor_tensor(dst, hsum[:, 8 * t:8 * t + 8, :], hsum[:, 8 * t + 1:8 * t + 9, :], ALU.add)\
                        .then_inc(box_half, 1)
                    pool.wait_ge(box_half, i + 1)
                    nc.gpsimd.tensor_tensor(dst, dst, hsum[:, 8 * t + 2:8 * t + 10, :], ALU.add).then_inc(box_done, 1)

                for t in range(CHUNKS):
                    across(0, t)
                    if t > 0:
                        down(0, 0, t - 1)
                down(0, 0, CHUNKS - 1)

                def image(n, b, last):
                    for u in range(UNITS):
                        t, oh = u // CH, u % CH
                        pool.wait_ge(affine_done, UNITS * n + u + 1)
                        v = xb[:, b, oh, CT * t:CT * t + CT]
                        nc.gpsimd.tensor_tensor(v, v, res[:, u % BANKS, :], ALU.add).then_inc(added, 1)
                        t = u - UNITS // 2
                        if t >= 1 and not last:
                            across(n + 1, t - 1)
                        if t >= 2 and not last:
                            down(n + 1, 1 - b, t - 2)
                    if not last:
                        across(n + 1, CHUNKS - 1)
                        down(n + 1, 1 - b, CHUNKS - 2)
                        down(n + 1, 1 - b, CHUNKS - 1)

                images(pool, image)

            @block.vector
            def _(dve):
                nc.vector.memset(sgn[:, :, :, :, :], -0.5)
                nc.vector.memset(beta[:, :, :], 0.0).then_inc(cleared, 1)
                dve.wait_ge(cleared, 1)
                for h in range(CH):
                    dve.wait_ge(kern_loaded, 16 * (h + 1))
                    nc.vector.tensor_scalar(ksgn[:, h, :, :], kern[:, :, :], 0.0, 0.5, ALU.is_gt, ALU.subtract)\
                        .then_inc(kern_signed, 1)
                dve.wait_ge(alpha_part, CH)
                nc.vector.tensor_copy(scale[:, :], ps_alpha[0][:, 0:CH]).then_inc(alpha_kept, 1)
                dve.wait_ge(alpha_kept, 1)
                nc.vector.tensor_tensor(scale[:, :], ps_alpha[1][:, 0:CH], scale[:, :], ALU.add).then_inc(alpha_kept, 1)
                dve.wait_ge(alpha_kept, 2)
                nc.vector.tensor_scalar(scale[:, :], scale[:, :], 4.0 / (TAPS * TAPS), None, ALU.mult)\
                    .then_inc(scale_made, 1)

                def signs(n, b, m):
                    dve.wait_ge(x_loaded[b], 16 * (m + 1))
                    at_least(dve, conv_full, UNITS * (n - 1)) if not isinstance(n, int) or n > 1 else None
                    for h in range(CH):
                        mean = tables[:, 2, bass.ds(n * CH + h, 1)]
                        nc.vector.tensor_scalar(sgn[:, b, h, 1:1 + H, 1:1 + W],
                                                xb[:, b, h, :].rearrange("p (r w) -> p r w", w=W), mean, 0.5,
                                                ALU.is_gt, ALU.subtract).then_inc(signed, 1)

                signs(0, 0, 0)

                def image(n, b, last):
                    for u in range(UNITS):
                        t = u // CH
                        i = UNITS * n + u
                        if u == UNITS // 2 and not last:
                            signs(n + 1, 1 - b, pair(n, b) + b)
                        dve.wait_ge(conv_full, i + 1)
                        dve.wait_ge(box_done, CHUNKS * n + t + 1)
                        at_least(dve, added, i - BANKS + 1) if not isinstance(i, int) or i >= BANKS else None
                        nc.vector.tensor_tensor(res[:, u % BANKS, :].rearrange("p (r w) -> p r w", w=W),
                                                ps_c[u % BANKS][:, :, :], box[:, b, 8 * t:8 * t + 8, :], ALU.mult)\
                            .then_inc(mult_done, 1)

                images(dve, image)


def layout(inputs, NI=8):
    f = lambda name: np.asarray(inputs[name])
    halves = lambda a: np.ascontiguousarray(a.reshape((CH, P) + a.shape[1:]).swapaxes(0, 1))
    per_block = lambda a: np.ascontiguousarray(np.tile(a, (Q, 1)))
    mean8 = np.kron(np.eye(P // GC), np.full((GC, GC), 1.0 / GC)).astype(np.float32)
    return {
        "x": np.ascontiguousarray(f("x")[:NI].reshape(NI, HW, C).swapaxes(1, 2)),
        "dww": halves(f("L0_conv_dw_w").reshape(TAPS, C).T),
        "dwb": halves(f("L0_conv_dw_b")),
        "omw": halves(f("L0_conv_om_w").reshape(C, G, 27).swapaxes(1, 2)),
        "omb": per_block(f("L0_conv_om_b").reshape(G, 27)),
        "vpw": halves(f("L0_conv_vp_w").reshape(C, G, GC).swapaxes(1, 2)),
        "vpb": per_block(f("L0_conv_vp_b").reshape(G, GC)),
        "opw": halves(f("L0_conv_op_w")),
        "vpw_c": halves(f("L0_conv_vp_w")),
        "vpb_c": halves(f("L0_conv_vp_b")),
        "kernel": halves(f("L1_conv_kernel").reshape(TAPS, C, C).swapaxes(0, 1)),
        "bias": halves(f("L1_conv_bias")),
        "ident": np.eye(P, dtype=np.float32),
        "mean8": mean8,
        "mean256": np.full((P, P), 1.0 / C, np.float32),
        "zeros": np.zeros((P, CH, 2, W), np.float32),
    }


def program(nc, d, out, NI=8):
    x2 = nc.dram_tensor("x2", (NI, C, HW), F32, kind="Internal").ap()
    with ExitStack() as ctx:
        sb = lambda name, shape, dt=F32: ctx.enter_context(nc.sbuf_tensor(name, shape, dt))
        consts = {"ident": sb("ident", [P, P]), "mean8": sb("mean8", [P, P]),
                  "minus1": sb("minus1", [P, 1]), "spare": sb("spare", [P, 8])}
        tables = sb("tables", [P, 3, NI * CH])
        mv2 = sb("mv2", [P, NI, CH, 2])
        reach = sb("reach", [P, 1])
        setup = ctx.enter_context(nc.semaphore("setup"))
        setup_v = ctx.enter_context(nc.semaphore("setup_v"))
        with nc.Block() as block:
            @block.sync
            def _(sp):
                sp.dma_start(consts["mean8"][:, :], d["mean8"]).then_inc(setup, 16)
                sp.wait_ge(setup, 16)

            @block.vector
            def _(dve):
                nc.vector.memset(consts["minus1"][:, :], -1.0).then_inc(setup_v, 1)
                dve.wait_ge(setup_v, 1)
        layer0_stats(nc, d["x"], consts, tables, NI)
        layer0(nc, d["x"], d["zeros"], d, x2, consts, tables, mv2, reach, NI)
        layer0_any_offset(nc, d["x"], d, x2, consts, tables, mv2, reach, NI)
        group_tables(nc, mv2, consts, tables, NI, "gt2_")
        layer1(nc, x2, d, out, consts, tables, NI)



def kernel(**inputs):
    import concourse.bacc as _bacc
    from concourse.bass_utils import run_bass_kernel_spmd as _run

    nc = _bacc.Bacc("TRN2", target_bir_lowering=False, num_devices=1)
    arrays, d = {}, {}
    for name, a in layout(inputs).items():
        arrays[f"in_{name}_dram"] = a
        d[name] = nc.dram_tensor(f"in_{name}_dram", a.shape, mybir.dt.from_np(a.dtype), kind="ExternalInput").ap()
    n = inputs["x"].shape[0]
    out = nc.dram_tensor("out_0_dram", (n, C, HW), F32, kind="ExternalOutput").ap()
    program(nc, d, out, n)
    r = _run(nc, [arrays], core_ids=[0])
    got = r.results[0]["out_0_dram"]
    return np.ascontiguousarray(got.reshape(n, C, H, W).transpose(0, 2, 3, 1))
```

```python
from contextlib import ExitStack

import concourse.bass as bass
import numpy as np
from concourse import mybir

F32 = mybir.dt.float32
BF16 = mybir.dt.bfloat16
ALU = mybir.AluOpType
ACT = mybir.ActivationFunctionType
AX_X = mybir.AxisListType.X

P = 128
H = W = 64
HW = H * W
C = 256
CH = C // P
G, GC = 32, 8
TAPS = 9
Q = P // G
QR = H // Q
SR = 4
STEPS = QR // SR
TOK = SR * W
WR = SR + 4
VR, VW = QR + 4, W + 4
D5 = 5
SHIFTS = D5 * D5
C_PE = 6
PE_SUMS = (C_PE - 1) * TOK + TOK // 4
PBUF = 4
PROD_BUF = 1
AHEAD_BUF = PBUF - 2
LATER = (SHIFTS - 1 - PROD_BUF) % PBUF
DW_UNITS = 4
V_UNITS = GC // 2
BG_IMG = STEPS * DW_UNITS + (STEPS + 1) * V_UNITS
GROUP = C // 32
KROWS, CB = 3 * 32, P // 32
FARTHEST = H - 1
EPS = 1e-5


def at_least(eng, sem, value):
    if not isinstance(value, int) or value > 0:
        eng.wait_ge(sem, value)


def bg_before(n, j):
    return n * BG_IMG + (0 if j == 0 else j * (DW_UNITS + V_UNITS) + V_UNITS)


def row_groups(j):
    return [0, 1] if j == 0 else [j + 1]


def shares(count, part, parts):
    return range(count * part // parts, count * (part + 1) // parts)


def first_stats(nc, x, consts, tables):
    PIECES = 4
    SIZE = HW // PIECES
    with ExitStack() as ctx:
        sb = lambda name, shape, dt=F32: ctx.enter_context(nc.sbuf_tensor(name, shape, dt))
        sem = lambda name: ctx.enter_context(nc.semaphore(name))
        xt = sb("st_x", [P, CH, HW])
        bs = sb("st_bs", [P, CH, HW // 512, 6])
        mv = sb("st_mv", [P, 1, CH, 2])
        x_loaded = [sem(f"st_loaded{i}") for i in range(CH * PIECES)]
        summed, aggregated = sem("st_summed"), sem("st_aggregated")
        with nc.Block() as block:
            @block.sync
            def _(sp):
                for h in range(CH):
                    for i in range(PIECES):
                        at = slice(SIZE * i, SIZE * (i + 1))
                        sp.dma_start(xt[:, h, at], x[0, P * h:P * h + P, at]).then_inc(x_loaded[PIECES * h + i], 16)

            @block.vector
            def _(dve):
                for h in range(CH):
                    for i in range(HW // 512):
                        if 512 * i % SIZE == 0:
                            dve.wait_ge(x_loaded[PIECES * h + 512 * i // SIZE], 16)
                        nc.vector.bn_stats(bs[:, h, i, :], xt[:, h, 512 * i:512 * i + 512]).then_inc(summed, 1)
                for h in range(CH):
                    dve.wait_ge(summed, HW // 512 * (h + 1))
                    nc.vector.bn_aggr(mv[:, 0, h, :], bs[:, h, :, :]).then_inc(aggregated, 1)
                dve.wait_ge(aggregated, CH)
        group_tables(nc, mv, consts, tables, 1, "gt1_")


def group_tables(nc, mv, consts, tables, NI, u):
    NS = NI * CH
    with ExitStack() as ctx:
        sb = lambda name, shape, dt=F32: ctx.enter_context(nc.sbuf_tensor(name, shape, dt))
        sem = lambda name: ctx.enter_context(nc.semaphore(name))
        mean = sb(u + "mean", [P, NS])
        var = sb(u + "var", [P, NS])
        ps = ctx.enter_context(nc.psum_tensor(u + "ps", [P, 2, 512], F32))
        v, pe_done, act_done = sem(u + "v"), sem(u + "pe"), sem(u + "act")
        with nc.Block() as block:
            @block.vector
            def _(dve):
                dve_steps = [0]

                def after(ins):
                    dve_steps[0] += 1
                    ins.then_inc(v, 1)
                    dve.wait_ge(v, dve_steps[0])

                flat = mv[:, :, :, :].rearrange("p n h s -> p (n h) s")
                after(nc.vector.tensor_copy(mean[:, :], flat[:, :, 0]))
                dve.wait_ge(pe_done, 1)
                gm = tables[:, 2, :]
                after(nc.vector.tensor_copy(gm, ps[:, 0, 0:NS]))
                after(nc.vector.tensor_tensor(mean[:, :], mean[:, :], gm, ALU.subtract))
                after(nc.vector.tensor_tensor(mean[:, :], mean[:, :], mean[:, :], ALU.mult))
                after(nc.vector.tensor_tensor(var[:, :], flat[:, :, 1], mean[:, :], ALU.add))
                dve.wait_ge(pe_done, 2)
                after(nc.vector.tensor_scalar(var[:, :], ps[:, 1, 0:NS], EPS, None, ALU.add))
                dve.wait_ge(act_done, 1)
                after(nc.vector.reciprocal(tables[:, 0, :], var[:, :]))
                after(nc.vector.scalar_tensor_tensor(out=tables[:, 1, :], in0=gm, scalar=-1.0,
                                                     in1=tables[:, 0, :], op0=ALU.mult, op1=ALU.mult))

            @block.tensor
            def _(pe):
                pe.wait_ge(v, 1)
                nc.tensor.matmul(ps[:, 0, 0:NS], consts["mean8"][:, :], mean[:, :],
                                 start=True, stop=True).then_inc(pe_done, 1)
                pe.wait_ge(v, 5)
                nc.tensor.matmul(ps[:, 1, 0:NS], consts["mean8"][:, :], var[:, :],
                                 start=True, stop=True).then_inc(pe_done, 1)

            @block.scalar
            def _(act):
                act.wait_ge(v, 6)
                nc.scalar.activation(var[:, :], var[:, :], ACT.Sqrt).then_inc(act_done, 1)


def tap_rects(ky, kx):
    if ky == 0 and kx == 0:
        return [(0, 3, 0, 3)], []
    if ky == 0:
        return [(0, 3, 2, 3)], [(0, 3, 0, 2)]
    if kx == 0:
        return [(2, 3, 0, 3)], [(0, 2, 0, 3)]
    return [(2, 3, 2, 3)], [(0, 2, 0, 3), (2, 3, 0, 2)]


def layer0(nc, x, zeros, w_dram, x2, consts, tables, mv2, reach, NI):
    with ExitStack() as ctx:
        sb = lambda name, shape, dt=F32: ctx.enter_context(nc.sbuf_tensor(name, shape, dt))
        psum = lambda name, shape: ctx.enter_context(nc.psum_tensor(name, shape, F32))
        sem = lambda name: ctx.enter_context(nc.semaphore(name))

        win = sb("win", [P, CH, Q, WR, W])
        xdw = sb("xdw", [P, CH, Q, TOK])
        val = sb("val", [P, GC, VR, VW])
        hat = sb("hat", [P, 2, 2, 3, TOK])
        msk = sb("msk", [P, 2, TOK])
        over = sb("over", [P, 2, TOK], BF16)
        over_sum = sb("over_sum", [P, 2, TAPS])
        over_max = sb("over_max", [P, 1])
        mwy = sb("mwy", [P, 2, 3, TOK])
        wsum = sb("wsum", [P, D5, D5, TOK])
        pv = sb("pv", [P, PBUF, GC, TOK])
        prod = pv[:, PROD_BUF, :, :].rearrange("p c t -> p (c t)")
        acc = sb("acc", [P, GC, TOK])
        acc_flat = acc[:, :, :].rearrange("p c t -> p (c t)")
        pv_flat = pv[:, :, :, :].rearrange("p b c t -> p b (c t)")
        acc_t = sb("acc_t", [P, CH, Q * TOK])
        xres = sb("xres", [P, CH, Q, TOK])
        tri = sb("tri", [P, CB, Q, SR, W])
        diag = sb("diag", [P, CH, CB, 3, 32])
        eye3 = sb("eye3", [P, 32])
        gx = sb("gx", [P, 2, CH])
        gx_tri = sb("gx_tri", [KROWS, CB, 2, CH])
        bs1 = sb("bs1", [P, CH, HW // 512, 6])
        mv1 = sb("mv1", [P, CH, 2])
        mean1 = sb("mean1", [P, CH])
        var1 = sb("var1", [P, CH])
        gn_tri = sb("gn_tri", [KROWS, 2, CB * 2, CH])
        omw = sb("omw", [P, CH, 27, G])
        vpw = sb("vpw", [P, CH, GC, G])
        opw = sb("opw", [P, CH, C])
        dww = sb("dww", [P, CH, CB, 3])
        dwb = sb("dwb", [P, CH])
        omb = sb("omb", [P, 27])
        nomb = sb("nomb", [P, 27])
        vpb = sb("vpb", [P, GC])
        mv_now = sb("mv_now", [P, CH, 2])
        gn = sb("gn", [P, 2, 2, CH])
        bs2 = sb("bs2", [P, CH, STEPS * 2, 6])

        ps_xy = psum("ps_xy", [P, 2, 2, TOK])
        ps_m = psum("ps_m", [P, 2, TOK])
        ps_bg = psum("ps_bg", [P, 2, 512])
        ps_add = psum("ps_add", [P, 3 * 512])

        weights_loaded, diag_made, val_zero = sem("weights_loaded"), sem("diag_made"), sem("val_zero")
        win_loaded, win_normed = sem("win_loaded"), sem("win_normed")
        tri_first_loaded = sem("tri_first_loaded")
        tri_loaded, tri_normed, gn_spread = sem("tri_loaded"), sem("tri_normed"), sem("gn_spread")
        bg_full, bg_free = sem("bg_full"), sem("bg_free")
        om_full, om_free, msk_free = sem("om_full"), sem("om_free"), sem("msk_free")
        abs_done, w0_done, hat_full = sem("abs_done"), sem("w0_done"), sem("hat_full")
        mwy_done, prod_done, wadd_done = sem("mwy_done"), sem("prod_done"), sem("wadd_done")
        pv_full, add_done, add_out = sem("pv_full"), sem("add_done"), sem("add_out")
        vadd_done, acc_begun = sem("vadd_done"), sem("acc_begun")
        acc_sent, xres_loaded = sem("acc_sent"), sem("xres_loaded")
        pj_full, pj_added, stats2 = sem("pj_full"), sem("pj_added"), sem("stats2")
        gn_kept = sem("gn_kept")
        x_ahead, sums_made, gx_step = sem("x_ahead"), sem("sums_made"), sem("gx_step")
        gx_mean, gx_root = sem("gx_mean"), sem("gx_root")
        MEANS_AT = C_PE * TOK - 2 * CH
        GX_STEPS = 11
        x2_stored, over_done, aggr2 = sem("x2_stored"), sem("over_done"), sem("aggr2")
        mv_kept = sem("mv_kept")
        WL = 16 * 9

        VALUES_AT = [3, 4, 5, 6, 7, 8]
        PROJECT_AT, PROJECTIONS = 8, range(4)
        STATS_AT = 2
        DW_AT = {0: 0, 1: 1, 8: 2, 9: 3}
        OFFSETS_AT = {11 + i: i for i in range(6)}

        def steps_of_images(eng, step):
            for j in range(STEPS):
                step(0, j, j == 0, False)
            if NI > 2:
                with eng.Fori(1, NI - 1) as n:
                    for j in range(STEPS):
                        step(n, j, False, False)
            for j in range(STEPS):
                step(NI - 1, j, False, j == STEPS - 1)

        tri_first = pv[:, AHEAD_BUF:PBUF, :, :].rearrange("p b c t -> p (b c t)")\
            .rearrange("p (c q r w) -> p c q r w", c=CB, q=Q, r=SR)

        def tri_of(n, j, h):
            return tri_first if isinstance(n, int) and (n, j, h) == (0, 0, 1) else tri

        def has_next(n):
            return not (isinstance(n, int) and n == NI - 1)

        def gx_made(n):
            return 1 if isinstance(n, int) and n == 0 else GX_STEPS * n

        def following(n, j):
            return (n, j + 1) if j < STEPS - 1 else (n + 1, 0)

        def previous(n, j):
            return (n, j - 1) if j > 0 else (n - 1, STEPS - 1)

        x_v = x.rearrange("n (h p) (r w) -> n p h r w", p=P, w=W)
        x2_v = x2.rearrange("n (h p) (r w) -> n p h r w", p=P, w=W)

        def image(v, n):
            return v[n] if isinstance(n, int) else v[bass.ds(n, 1)].rearrange("n p h r w -> p (n h) r w")

        def window_edge(q, j):
            lo = QR * q + SR * j - 2
            return max(0, -lo), WR - max(0, lo + WR - H)

        with nc.Block() as block:
            @block.sync
            def _(sp):
                def spread_scales(n):
                    sp.wait_ge(gx_step, gx_made(n))
                    for ky in range(3):
                        for c in range(CB):
                            sp.dma_start(gx_tri[32 * ky:32 * ky + 32, c, :, :], gx[32 * c:32 * c + 32, :, :])\
                                .then_inc(gn_spread, 16)

                def load_window(n, j):
                    if not (isinstance(n, int) and n == 0 and j == 0):
                        n0, j0 = previous(n, j)
                        sp.wait_ge(bg_full, bg_before(n0, j0) + V_UNITS * len(row_groups(j0)))
                    for q in range(Q):
                        lo, hi = window_edge(q, j)
                        if j > 0:
                            lo = SR
                        r0 = QR * q + SR * j - 2
                        sp.dma_start(win[:, :, q, lo:hi, :], image(x_v, n)[:, :, r0 + lo:r0 + hi, :])\
                            .then_inc(win_loaded, 16)
                    if j == 0:
                        sp.dma_start(win[:, :, 0, 0:2, :], zeros).then_inc(win_loaded, 16)
                    elif j == STEPS - 1:
                        sp.dma_start(win[:, :, Q - 1, WR - 2:WR, :], zeros).then_inc(win_loaded, 16)

                def load_tri(n, j, h):
                    dst_all = tri_of(n, j, h)
                    loaded = tri_first_loaded if dst_all is tri_first else tri_loaded
                    if h == 0:
                        at_least(sp, bg_full, bg_before(n, j))
                    elif dst_all is tri:
                        sp.wait_ge(bg_full, bg_before(n, j) + V_UNITS * len(row_groups(j)) + DW_UNITS // 2)
                    for ky in range(3):
                        dst = dst_all[32 * ky:32 * ky + 32, :, :, :, :]
                        r0 = SR * j + ky - 1
                        src = image(x_v, n)[:, h].rearrange("(c p) r w -> p c r w", p=32)
                        for q in range(Q):
                            lo, hi = max(0, -(QR * q + r0)), min(SR, H - (QR * q + r0))
                            sp.dma_start(dst[:, :, q, lo:hi, :],
                                         src[:, :, QR * q + r0 + lo:QR * q + r0 + hi, :]).then_inc(loaded, 16)
                    zero_rows = zeros[0:32].rearrange("p h r w -> p (h r) w")
                    if j == 0:
                        sp.dma_start(dst_all[0:32, :, 0, 0, :], zero_rows).then_inc(loaded, 16)
                    elif j == STEPS - 1:
                        sp.dma_start(dst_all[64:96, :, Q - 1, SR - 1, :], zero_rows).then_inc(loaded, 16)

                def send_acc(n, j):
                    s = STEPS * n + j
                    at_least(sp, x2_stored, 16 * Q * s)
                    sp.wait_ge(vadd_done, (SHIFTS) * (s + 1))
                    sp.wait_ge(add_out, s + 1)
                    for q in range(Q):
                        for h in range(CH):
                            g0 = G * q + h * (G // CH)
                            sp.dma_start(acc_t[:, h, q * TOK:(q + 1) * TOK], acc[g0:g0 + G // CH, :, :])\
                                .then_inc(acc_sent, 16)
                    for q in range(Q):
                        r0 = QR * q + SR * j
                        sp.dma_start(xres[:, :, q, :].rearrange("p h (r w) -> p h r w", w=W),
                                     image(x_v, n)[:, :, r0:r0 + SR, :]).then_inc(xres_loaded, 16)

                def store_x2(n, j):
                    s = STEPS * n + j
                    sp.wait_ge(stats2, 4 * (s + 1))
                    for q in range(Q):
                        r0 = QR * q + SR * j
                        sp.dma_start(image(x2_v, n)[:, :, r0:r0 + SR, :],
                                     xres[:, :, q, :].rearrange("p h (r w) -> p h r w", w=W))\
                            .then_inc(x2_stored, 16)

                spread_scales(0)
                load_window(0, 0)
                load_tri(0, 0, 0)
                for dst, name in ((dww, "dww3"), (eye3, "eye3"), (dwb, "dwb"), (omw, "omw"), (omb, "omb"), (vpw, "vpw"),
                                  (vpb, "vpb"), (opw, "opw")):
                    sp.dma_start(dst[:], w_dram[name]).then_inc(weights_loaded, 16)
                sp.dma_start(consts["ident"][:, :], w_dram["ident"]).then_inc(weights_loaded, 16)
                load_tri(0, 0, 1)
                load_window(0, 1)
                load_tri(0, 1, 0)

                def step(n, j, first, last):
                    if not first:
                        send_acc(*previous(n, j))
                    if j < CH and has_next(n):
                        src = (x_v[n + 1] if isinstance(n, int) else image(x_v, n + 1))[:, j]
                        sp.dma_start(pv_flat[:, AHEAD_BUF:PBUF, :], src.rearrange("p r w -> p (r w)")
                                     .rearrange("p (b t) -> p b t", b=2)).then_inc(x_ahead, 16)
                    n2, j2 = following(*following(n, j))
                    more = not (isinstance(n, int) and n == NI - 1 and j >= STEPS - 2)
                    if more:
                        load_window(n2, j2)
                    if not last:
                        load_tri(*following(n, j), 1)
                    if more:
                        load_tri(n2, j2, 0)
                    if j == STEPS - 2 and has_next(n):
                        spread_scales(n + 1)
                    if not first:
                        store_x2(*previous(n, j))

                steps_of_images(sp, step)
                send_acc(NI - 1, STEPS - 1)
                store_x2(NI - 1, STEPS - 1)
                sp.wait_ge(x2_stored, 16 * Q * STEPS * NI)

            def loads_before(n, j):
                return n * (STEPS * Q + 2) + j * Q + (1 if j > 0 else 0)

            def tri_loads_before(n, j, h):
                each = lambda j: 3 * Q + (1 if j in (0, STEPS - 1) else 0)
                return n * 2 * sum(each(i) for i in range(STEPS)) + 2 * sum(each(i) for i in range(j)) + h * each(j) \
                    - (0 if isinstance(n, int) and (n, j) == (0, 0) else each(0))

            @block.scalar
            def _(act):

                def normalise(n, j):
                    n_loads = Q + (1 if j in (0, STEPS - 1) else 0)
                    if j == 0:
                        act.wait_ge(gx_step, gx_made(n))
                        act.wait_ge(gn_spread, 16 * 3 * CB * (n + 1))
                    nc.scalar.activation(gn[:, j % 2, :, :], gx[:, :, :], ACT.Copy).then_inc(gn_kept, 1)
                    nc.scalar.activation(gn_tri[:, j % 2, :, :], gx_tri[:, :, :, :].rearrange("p c s n -> p (c s) n"),
                                         ACT.Copy).then_inc(gn_kept, 1)
                    act.wait_ge(gn_kept, 2 * (STEPS * n + j + 1))
                    act.wait_ge(win_loaded, 16 * (loads_before(n, j) + n_loads))
                    for h in range(CH):
                        scale, shift = gn[:, j % 2, 0, h:h + 1], gn[:, j % 2, 1, h:h + 1]
                        parts = [(0, Q, SR, WR)]
                        if j == 0:
                            parts = [(0, 1, 2, WR), (1, Q, 0, WR)]
                        elif j == STEPS - 1:
                            parts = [(0, Q - 1, SR, WR), (Q - 1, Q, SR, WR - 2)]
                        for q0, q1, r0, r1 in parts:
                            v = win[:, h, q0:q1, r0:r1, :]
                            last = nc.scalar.activation(v, v, ACT.Identity, bias=shift, scale=scale)
                    last.then_inc(win_normed, 1)

                def normalise_tri(n, j, h):
                    loads = 3 * Q + (1 if j in (0, STEPS - 1) else 0)
                    if tri_of(n, j, h) is tri_first:
                        act.wait_ge(tri_first_loaded, 16 * loads)
                    else:
                        act.wait_ge(tri_loaded, 16 * (tri_loads_before(n, j, h) + loads))
                    parts = [(0, KROWS, 0, Q, 0, SR)]
                    if j == 0:
                        parts = [(0, KROWS, 0, 1, 1, SR), (32, 64, 0, 1, 0, 1), (64, KROWS, 0, 1, 0, 1),
                                 (0, KROWS, 1, Q, 0, SR)]
                    elif j == STEPS - 1:
                        parts = [(0, KROWS, 0, Q - 1, 0, SR), (0, KROWS, Q - 1, Q, 0, SR - 1),
                                 (0, 64, Q - 1, Q, SR - 1, SR)]
                    for c in range(CB):
                        for p0, p1, q0, q1, r0, r1 in parts:
                            v = tri_of(n, j, h)[p0:p1, c, q0:q1, r0:r1, :]
                            last = nc.scalar.activation(v, v, ACT.Identity, bias=gn_tri[p0:p1, j % 2, 2 * c + 1, h:h + 1],
                                                        scale=gn_tri[p0:p1, j % 2, 2 * c, h:h + 1])
                    last.then_inc(tri_normed, 1)

                def keep_depthwise(n, j, h):
                    for u in range(2 * h, 2 * h + 2):
                        qp = u % 2
                        act.wait_ge(bg_full, bg_before(n, j) + V_UNITS * len(row_groups(j)) + u + 1)
                        nc.scalar.activation(xdw[:, h, 2 * qp:2 * qp + 2, :], ps_bg[:, u % 2, :], ACT.Identity,
                                             bias=dwb[:, h:h + 1]).then_inc(bg_free, 1)

                def keep_values(n, j, part, parts):
                    s = STEPS * n + j
                    if part == 0 and (not isinstance(s, int) or s > 2):
                        act.wait_ge(vadd_done, SHIFTS * (s - 2))
                    for i in shares(V_UNITS * len(row_groups(j)), part, parts):
                        g, cp, par = row_groups(j)[i // V_UNITS], i % V_UNITS, i % 2
                        unit = bg_before(n, j) + i
                        act.wait_ge(bg_full, unit + 1)
                        for c in (2 * cp, 2 * cp + 1):
                            src = ps_bg[:, par, (c % 2) * TOK:(c % 2 + 1) * TOK].rearrange("p (r w) -> p r w", w=W)
                            parts = [(0, P, 0, SR)]
                            if g == 0:
                                parts = [(0, G, 2, SR), (G, 2 * G, 0, SR), (2 * G, P, 0, SR)]
                            elif g == STEPS:
                                parts = [(0, 2 * G, 0, SR), (2 * G, 3 * G, 0, SR), (3 * G, P, 0, 2)]
                            for p0, p1, r0, r1 in parts:
                                last = nc.scalar.activation(
                                    val[p0:p1, c, SR * g + r0:SR * g + r1, 2:2 + W], src[p0:p1, r0:r1, :],
                                    ACT.Identity, bias=vpb[p0:p1, c:c + 1])
                        last.then_inc(bg_free, 1)

                def hats(n, j, k):
                    t = (STEPS * n + j) * TAPS + k
                    par = (j + k) % 2
                    act.wait_ge(om_full, t + 1)
                    at_least(act, prod_done, t - 1)
                    nc.scalar.activation(msk[:, par, :], ps_m[:, 0, :], ACT.Identity,
                                         bias=omb[:, 18 + k:19 + k]).then_inc(msk_free, 1)
                    for a in range(2):
                        d, b, nb = ps_xy[:, par, a, :], omb[:, 2 * k + a:2 * k + a + 1], nomb[:, 2 * k + a:2 * k + a + 1]
                        nc.scalar.activation(hat[:, par, a, 1, :], d, ACT.Abs, bias=b).then_inc(abs_done, 1)
                    for a in range(2):
                        d, b, nb = ps_xy[:, par, a, :], omb[:, 2 * k + a:2 * k + a + 1], nomb[:, 2 * k + a:2 * k + a + 1]
                        nc.scalar.activation(hat[:, par, a, 0, :], d, ACT.Relu, bias=nb, scale=-1.0)
                        last = nc.scalar.activation(hat[:, par, a, 2, :], d, ACT.Relu, bias=b)
                    last.then_inc(om_free, 1)
                    act.wait_ge(abs_done, 1 + 2 * (t + 1))
                    if k == 0:
                        at_least(act, over_done, STEPS * n + j - 1)
                    nc.scalar.activation(over[:, :, :], hat[:, par, :, 1, :], ACT.Relu, bias=consts["minus1"][:, 0:1],
                                         accum_out=over_sum[:, j % 2, k:k + 1]).then_inc(w0_done, 1)
                    act.wait_ge(w0_done, t + 1)
                    nc.scalar.activation(hat[:, par, :, 1, :], hat[:, par, :, 1, :], ACT.Copy, bias=1.0,
                                         scale=-1.0).then_inc(hat_full, 1)

                def keep_x2(n, j, u):
                    oh, tb = u // 2, u % 2
                    act.wait_ge(pj_full, 4 * (STEPS * n + j) + u + 1)
                    nc.scalar.activation(xres[:, oh, 2 * tb:2 * tb + 2, :].rearrange("p q t -> p (q t)"),
                                         ps_bg[:, u % 2, :], ACT.Copy).then_inc(pj_added, 1)

                def summed(n, j):
                    s = STEPS * n + j
                    act.wait_ge(add_done, SHIFTS * (s + 1))
                    at_least(act, acc_sent, 16 * CH * Q * s)
                    nc.scalar.activation(acc_flat[:, 0:PE_SUMS], ps_add[:, 0:PE_SUMS], ACT.Copy).then_inc(add_out, 1)

                normalise(0, 0)
                act.wait_ge(val_zero, 6)
                normalise_tri(0, 0, 0)
                act.wait_ge(weights_loaded, WL)
                nc.scalar.mul(nomb[:, :], omb[:, :], -1.0).then_inc(abs_done, 1)
                act.wait_ge(abs_done, 1)
                keep_values(0, 0, 0, 1)
                normalise_tri(0, 0, 1)
                keep_depthwise(0, 0, 0)
                keep_depthwise(0, 0, 1)
                hats(0, 0, 0)
                hats(0, 0, 1)

                def step(n, j, first, last):
                    if not last:
                        n1, j1 = following(n, j)
                        n2, j2 = following(n1, j1)
                    more = not (isinstance(n, int) and n == NI - 1 and j >= STEPS - 2)
                    for k in range(2, TAPS):
                        hats(n, j, k)
                        if first and k == 2:
                            normalise(0, 1)
                        if first and k == 5:
                            normalise_tri(0, 1, 0)
                        if not last:
                            if k in VALUES_AT:
                                keep_values(n1, j1, VALUES_AT.index(k), len(VALUES_AT))
                        if not first:
                            for u in PROJECTIONS if k == PROJECT_AT else []:
                                keep_x2(*previous(n, j), u)
                    if not last:
                        if j == STEPS - 2 and has_next(n):
                            act.wait_ge(gx_step, GX_STEPS * n + 9)
                            nc.scalar.activation(var1[:, :], var1[:, :], ACT.Sqrt).then_inc(gx_root, 1)
                        keep_depthwise(n1, j1, 0)
                        normalise_tri(n1, j1, 1)
                        keep_depthwise(n1, j1, 1)
                        if more:
                            normalise(n2, j2)
                        hats(n1, j1, 0)
                        hats(n1, j1, 1)
                        if more:
                            normalise_tri(n2, j2, 0)
                    summed(n, j)

                steps_of_images(act, step)
                for u in range(4):
                    keep_x2(NI - 1, STEPS - 1, u)

            @block.tensor
            def _(pe):
                pe.wait_ge(weights_loaded, WL)

                def depthwise(n, j, u):
                    h, qp = u // 2, u % 2
                    s = STEPS * n + j
                    if qp == 0:
                        pe.wait_ge(tri_normed, CH * s + h + 1)
                    if u >= 2 or (isinstance(s, int) and s < 2):
                        pe.wait_ge(bg_free, bg_before(n, j) + V_UNITS * len(row_groups(j)) + u - 1)
                    else:
                        pe.wait_ge(pj_added, 4 * (s - 2) + u + 3)
                    for kx in (1, 0, 2):
                        o0, o1 = max(0, 1 - kx), W - max(0, kx - 1)
                        for c in range(CB):
                            out = ps_bg[32 * c:32 * c + 32, u % 2, :].rearrange("p (q r w) -> p q r w", q=2, w=W)
                            src = tri_of(n, j, h)[:, c, 2 * qp:2 * qp + 2, :, o0 + kx - 1:o1 + kx - 1]
                            mm = nc.tensor.matmul(out[:, :, :, o0:o1], diag[:, h, c, kx, :], src,
                                                  start=kx == 1, stop=kx == 2)
                    mm.then_inc(bg_full, 1)

                def values(n, j, i, ci):
                    g, cp, u = row_groups(j)[i // V_UNITS], i % V_UNITS, i
                    bank, c = u % 2, 2 * cp + ci
                    r0 = 0 if g == 0 else SR
                    if u == 0 and ci == 0:
                        pe.wait_ge(win_normed, STEPS * n + j + 1)
                    if ci == 0:
                        at_least(pe, bg_free, bg_before(n, j) + u - 1)
                    for h in range(CH):
                        for q in range(Q):
                            mm = nc.tensor.matmul(ps_bg[G * q:G * q + G, bank, ci * TOK:(ci + 1) * TOK],
                                                  vpw[:, h, c, :], win[:, h, q, r0:r0 + SR, :],
                                                  start=h == 0, stop=h == CH - 1)
                    if ci == 1:
                        mm.then_inc(bg_full, 1)

                def offsets(n, j, k, part=None):
                    t = (STEPS * n + j) * TAPS + k
                    par = (j + k) % 2
                    for i in range(3) if part is None else [part]:
                        if i == 0:
                            if k == 0:
                                pe.wait_ge(bg_free, bg_before(*following(n, j)))
                            at_least(pe, om_free, t - 1)
                        comp = (2 * k, 2 * k + 1, 18 + k)[i]
                        dst = (ps_xy[:, par, 0, :], ps_xy[:, par, 1, :], ps_m[:, 0, :])[i]
                        if i == 2:
                            at_least(pe, msk_free, t)
                        for h in range(CH):
                            for q in range(Q):
                                mm = nc.tensor.matmul(dst[G * q:G * q + G, :], omw[:, h, comp, :], xdw[:, h, q, :],
                                                      start=h == 0, stop=h == CH - 1)
                    if part in (None, 2):
                        mm.then_inc(om_full, 1)

                def project(n, j, u, tail=False):
                    s = STEPS * n + j
                    oh, tb = u // 2, u % 2
                    if u == 0:
                        pe.wait_ge(acc_sent, 16 * CH * Q * (s + 1))
                        pe.wait_ge(xres_loaded, 16 * Q * (s + 1))
                    if tail or u >= 2:
                        at_least(pe, pj_added, 4 * s + u - 1)
                    else:
                        pe.wait_ge(bg_free, bg_before(*following(*following(*following(n, j)))) - DW_UNITS + u - 1)
                    for h in range(CH):
                        nc.tensor.matmul(ps_bg[:, u % 2, :], opw[:, h, P * oh:P * oh + P],
                                         acc_t[:, h, 512 * tb:512 * tb + 512], start=h == 0, stop=False)
                    nc.tensor.matmul(ps_bg[:, u % 2, :], consts["ident"][:, :],
                                     xres[:, oh, 2 * tb:2 * tb + 2, :].rearrange("p q t -> p (q t)"),
                                     start=False, stop=True).then_inc(pj_full, 1)

                def all_values(n, j, part, parts):
                    for i in shares(V_UNITS * len(row_groups(j)), part, parts):
                        for ci in range(2):
                            values(n, j, i, ci)

                def step(n, j, first, last):
                    s = STEPS * n + j

                    def group_mean(i, src):
                        pe.wait_ge(gx_step, GX_STEPS * n + (4, 8)[i])
                        pe.wait_ge(add_out, s)
                        nc.tensor.matmul(ps_add[:, MEANS_AT + CH * i:MEANS_AT + CH * i + CH], consts["mean8"][:, :], src[:, :],
                                         start=True, stop=True).then_inc(gx_mean, 1)

                    for k in range(2, TAPS):
                        if j == STEPS - 2 and has_next(n) and k in (5, 8):
                            group_mean(k // 8, mean1 if k == 5 else var1)
                        offsets(n, j, k)
                        if not last:
                            if k in VALUES_AT:
                                all_values(*following(n, j), VALUES_AT.index(k), len(VALUES_AT))
                        if not first:
                            for u in PROJECTIONS if k == PROJECT_AT else []:
                                project(*previous(n, j), u, last)
                    for uv in range(SHIFTS):
                        if not last and uv in DW_AT:
                            depthwise(*following(n, j), DW_AT[uv])
                        if not last and uv in OFFSETS_AT:
                            offsets(*following(n, j), OFFSETS_AT[uv] // 3, OFFSETS_AT[uv] % 3)
                        pe.wait_ge(pv_full, SHIFTS * s + uv + 1)
                        if uv == 0:
                            at_least(pe, add_out, s)
                        for i in range(0, PE_SUMS, 512):
                            at = slice(i, min(i + 512, PE_SUMS))
                            mm = nc.tensor.matmul(ps_add[:, at], consts["ident"][:, :], pv_flat[:, uv % PBUF, at],
                                                  start=uv == 0, stop=uv == SHIFTS - 1)
                        mm.then_inc(add_done, 1)

                all_values(0, 0, 0, 1)
                pe.wait_ge(diag_made, CH * CB * 3)
                for u in range(DW_UNITS):
                    depthwise(0, 0, u)
                for k in range(2):
                    offsets(0, 0, k)
                steps_of_images(pe, step)
                for u in range(4):
                    project(NI - 1, STEPS - 1, u, True)

            @block.vector
            def _(dve):
                nc.vector.tensor_copy(gx[:, :, :], tables[:, 0:2, 0:CH]).then_inc(gx_step, 1)
                for v in (tri, tri_first):
                    nc.vector.memset(v[KROWS:P, :, :, :, :], 0.0).then_inc(val_zero, 1)
                for v in (val[:, :, :, 0:2], val[:, :, :, VW - 2:VW]):
                    nc.vector.memset(v, 0.0).then_inc(val_zero, 1)
                dve.wait_ge(val_zero, 4)
                for v in (val[0:G, :, 0:2, :], val[P - G:P, :, VR - 2:VR, :]):
                    nc.vector.memset(v, 0.0).then_inc(val_zero, 1)
                dve.wait_ge(weights_loaded, WL)
                for h in range(CH):
                    for c in range(CB):
                        for kx in range(3):
                            nc.vector.tensor_scalar(diag[:, h, c, kx, :], eye3[:, :], dww[:, h, c, kx:kx + 1], None,
                                                    ALU.mult).then_inc(diag_made, 1)
                nc.vector.memset(over_max[:, :], 0.0).then_inc(diag_made, 1)
                dve.wait_ge(diag_made, CH * CB * 3 + 1)
                def sums_ahead(n, j):
                    dve.wait_ge(x_ahead, 16 * (CH * n + j + 1))
                    for i in range(HW // 512):
                        at = 512 * i % (GC * TOK)
                        last = nc.vector.bn_stats(bs1[:, j, i, :],
                                                  pv_flat[:, AHEAD_BUF + 512 * i // (GC * TOK), at:at + 512])
                    last.then_inc(sums_made, 1)

                def scales_ahead(n, part):
                    def after(i, ins):
                        ins.then_inc(gx_step, 1)
                        dve.wait_ge(gx_step, GX_STEPS * n + 1 + i)

                    gm = mv1[:, :, 0]
                    if part == 0:
                        for h in range(CH):
                            nc.vector.bn_aggr(mv1[:, h, :], bs1[:, h, :, :]).then_inc(gx_step, 1)
                        dve.wait_ge(gx_step, GX_STEPS * n + 1 + CH)
                        after(3, nc.vector.tensor_copy(mean1[:, :], mv1[:, :, 0]))
                    elif part == 1:
                        dve.wait_ge(gx_mean, 2 * n + 1)
                        after(4, nc.vector.tensor_copy(gm, ps_add[:, MEANS_AT:MEANS_AT + CH]))
                        after(5, nc.vector.tensor_tensor(mean1[:, :], mean1[:, :], gm, ALU.subtract))
                        after(6, nc.vector.tensor_tensor(mean1[:, :], mean1[:, :], mean1[:, :], ALU.mult))
                        after(7, nc.vector.tensor_tensor(var1[:, :], mv1[:, :, 1], mean1[:, :], ALU.add))
                    elif part == 2:
                        dve.wait_ge(gx_mean, 2 * n + 2)
                        after(8, nc.vector.tensor_scalar(var1[:, :], ps_add[:, MEANS_AT + CH:MEANS_AT + 2 * CH], EPS, None, ALU.add))
                    else:
                        dve.wait_ge(gx_root, n + 1)
                        dve.wait_ge(gn_kept, 2 * STEPS * (n + 1))
                        after(9, nc.vector.reciprocal(gx[:, 0, :], var1[:, :]))
                        after(10, nc.vector.scalar_tensor_tensor(out=gx[:, 1, :], in0=gm, scalar=-1.0,
                                                                 in1=gx[:, 0, :], op0=ALU.mult, op1=ALU.mult))
                        after(11, nc.vector.tensor_scalar(tables[:, 0:2, bass.ds((n + 1) * CH, CH)], gx[:, :, :], 1.0, None,
                                                          ALU.mult))

                def weights(n, j, first):
                    s = STEPS * n + j
                    ws = wsum[:, :, :, :]
                    at_least(dve, pv_full, SHIFTS * s)

                    def mask_rows(k):
                        t, par = TAPS * s + k, (j + k) % 2
                        dve.wait_ge(hat_full, t + 1)
                        nc.vector.tensor_tensor(mwy[:, par, :, :], hat[:, par, 1, :, :],
                                                msk[:, par, :].unsqueeze(1).to_broadcast([P, 3, TOK]), ALU.mult)\
                            .then_inc(mwy_done, 1)

                    def product(dst, k, rect):
                        a, b, c, d = rect
                        par = (j + k) % 2
                        shape = [P, b - a, d - c, TOK]
                        return nc.vector.tensor_tensor(
                            dst, hat[:, par, 0, c:d, :].unsqueeze(1).to_broadcast(shape),
                            mwy[:, par, a:b, :].unsqueeze(2).to_broadcast(shape), ALU.mult)

                    def in_prod(rect):
                        a, b, c, d = rect
                        at = 6 * TOK if a == 2 and d - c == 2 else 0
                        return prod[:, at:at + (b - a) * (d - c) * TOK].rearrange("p (a b t) -> p a b t", a=b - a, b=d - c)

                    mask_rows(0)
                    for k in range(TAPS):
                        t = TAPS * s + k
                        ky, kx = k // 3, k % 3
                        new, old = tap_rects(ky, kx)
                        dve.wait_ge(mwy_done, t + 1)
                        if k == 1:
                            at_least(dve, add_done, SHIFTS * s - LATER if not isinstance(s, int) or s > 0 else 0)
                            at_least(dve, vadd_done, SHIFTS * s)
                        if k > 1:
                            dve.wait_ge(wadd_done, (TAPS - 1) * s + k - 1)
                        for rect in old:
                            product(in_prod(rect), k, rect)
                        for a, b, c, d in new:
                            ins = product(ws[:, ky + a:ky + b, kx + c:kx + d, :], k, (a, b, c, d))
                        ins.then_inc(prod_done, 1)
                        if k + 1 < TAPS:
                            mask_rows(k + 1)
                        dve.wait_ge(prod_done, t + 1)
                        for a, b, c, d in old:
                            w = ws[:, ky + a:ky + b, kx + c:kx + d, :]
                            ins = nc.vector.tensor_tensor(w, w, in_prod((a, b, c, d)), ALU.add)
                        if k > 0:
                            ins.then_inc(wadd_done, 1)
                        if j == STEPS - 2 and has_next(n) and k in (1, 4, 8):
                            scales_ahead(n, (1, 4, 8).index(k))
                    if j < CH and has_next(n):
                        sums_ahead(n, j)
                    dve.wait_ge(wadd_done, (TAPS - 1) * (s + 1))

                def sample(n, j, first):
                    s = STEPS * n + j
                    dve.wait_ge(bg_free, bg_before(*following(n, j)))
                    at_least(dve, acc_sent, 16 * CH * Q * s)

                    def multiply(uv):
                        u, v = uv // D5, uv % D5
                        if uv == AHEAD_BUF and j < CH and has_next(n):
                            dve.wait_ge(sums_made, CH * n + j + 1)
                        if not isinstance(s, int) or s > 0 or uv >= PBUF:
                            dve.wait_ge(add_done, SHIFTS * s + uv - PBUF + 1)
                        for c0, c1, dst in ([(0, C_PE, pv[:, 0, 0:C_PE, :]), (C_PE, GC, acc[:, C_PE:GC, :])] if uv == 0
                                            else [(0, GC, pv[:, uv % PBUF, :, :])]):
                            w_in = wsum[:, u, v, :].rearrange("p (r w) -> p r w", w=W).unsqueeze(1)\
                                .to_broadcast([P, c1 - c0, SR, W])
                            nc.vector.tensor_tensor(dst.rearrange("p c (r w) -> p c r w", w=W),
                                                    val[:, c0:c1, SR * j + u:SR * j + u + SR, v:v + W], w_in, ALU.mult)\
                                .then_inc(acc_begun if c0 > 0 else pv_full, 1)

                    def add(uv):
                        a = acc_flat[:, PE_SUMS:]
                        dve.wait_ge(pv_full, SHIFTS * s + uv + 1)
                        p = pv_flat[:, uv % PBUF, PE_SUMS:]
                        if uv == 0:
                            at = slice(PE_SUMS, C_PE * TOK)
                            ins = nc.vector.tensor_copy(acc_flat[:, at], pv_flat[:, 0, at])
                        else:
                            if uv == 1:
                                dve.wait_ge(acc_begun, s + 1)
                            dve.wait_ge(vadd_done, SHIFTS * s + uv)
                            ins = nc.vector.tensor_tensor(a, a, p, ALU.add)
                        ins.then_inc(vadd_done, 1)

                    multiply(0)
                    for uv in range(SHIFTS):
                        if uv + 1 < SHIFTS:
                            multiply(uv + 1)
                        add(uv)
                        if uv == 4 and j == STEPS - 2 and has_next(n):
                            scales_ahead(n, 3)
                        if uv == STATS_AT:
                            if j == 1 and not (isinstance(n, int) and n == 0):
                                aggregate(n - 1)
                            if not first:
                                statistics(*previous(n, j))

                def statistics(n, j):
                    s = STEPS * n + j
                    dve.wait_ge(pj_added, 4 * (s + 1))
                    for u in range(4):
                        oh, tb = u // 2, u % 2
                        nc.vector.bn_stats(bs2[:, oh, 2 * j + tb, :], xres[:, oh, 2 * tb:2 * tb + 2, :].rearrange("p q t -> p (q t)"))\
                            .then_inc(stats2, 1)

                def aggregate(n):
                    for h in range(CH):
                        nc.vector.bn_aggr(mv_now[:, h, :], bs2[:, h, :, :]).then_inc(aggr2, 1)
                    dve.wait_ge(aggr2, CH * (n + 1))
                    nc.vector.tensor_scalar(mv2[:, bass.ds(n, 1), :, :].rearrange("p n h s -> p (n h s)"),
                                            mv_now[:, :, :].rearrange("p h s -> p (h s)"), 1.0, None,
                                            ALU.mult).then_inc(mv_kept, 1)

                def reach_of(n, j):
                    s = STEPS * n + j
                    nc.vector.tensor_reduce(consts["scratch"][:, j % 2:j % 2 + 1], over_sum[:, j % 2, :], AX_X, ALU.max)\
                        .then_inc(over_done, 1)
                    dve.wait_ge(over_done, s + 1)
                    nc.vector.tensor_tensor(over_max[:, :], over_max[:, :], consts["scratch"][:, j % 2:j % 2 + 1], ALU.max)

                def step(n, j, first, last):
                    weights(n, j, first)
                    reach_of(n, j)
                    sample(n, j, first)

                steps_of_images(dve, step)
                statistics(NI - 1, STEPS - 1)
                dve.wait_ge(stats2, 4 * STEPS * NI)
                dve.wait_ge(mv_kept, NI - 1)
                aggregate(NI - 1)
                dve.wait_ge(mv_kept, NI)
                nc.vector.tensor_copy(reach[:, :], over_max[:, :]).then_inc(over_done, 1)
                dve.wait_ge(over_done, STEPS * NI + 1)


def layer0_any_offset(nc, x, w_dram, x2, consts, tables, mv2, reach, NI):
    R = FARTHEST
    PADH = H + 2 * R
    vpad = nc.dram_tensor("vpad", (C, PADH, PADH), F32, kind="Internal").ap()
    CT = 512
    with ExitStack() as ctx:
        sb = lambda name, shape, dt=F32: ctx.enter_context(nc.sbuf_tensor(name, shape, dt))
        sem = lambda name: ctx.enter_context(nc.semaphore(name))
        xi = sb("g_x", [P, CH, HW])
        xpad = sb("g_xpad", [P, CH, H + 2, W + 2])
        xdw = sb("g_xdw", [P, CH, HW])
        xdw_step = xi[:, :, 0:Q * TOK].rearrange("p h (q t) -> p h q t", q=Q)
        prj = xi[:, :, Q * TOK:2 * Q * TOK].rearrange("p h (q t) -> p h q t", q=Q)
        off = sb("g_off", [P, 3, TAPS, TOK])
        wx = sb("g_wx", [P, TAPS, TOK])
        wy = sb("g_wy", [P, TAPS, TOK])
        rows = sb("g_rows", [P, GC, SR, PADH])
        acc = sb("g_acc", [P, GC, TOK])
        tmp = sb("g_tmp", [P, GC, TOK])
        acc_t = tmp[:, :, :].rearrange("p c t -> p (c t)").rearrange("p (h t) -> p h t", h=CH)
        xres = acc[:, :, :].rearrange("p c t -> p (c t)").rearrange("p (h q t) -> p h q t", h=CH, q=Q)
        w = sb("g_w", [P, TOK])
        at_y = sb("g_at_y", [P, 1])
        at_x = sb("g_at_x", [P, 1])
        gn = sb("g_gn", [P, 2, CH])
        bs = sb("g_bs", [P, CH, HW // CT, 6])
        mv_now = sb("g_mv", [P, CH, 2])
        omw = sb("g_omw", [P, CH, 27, G])
        vpw = sb("g_vpw", [P, CH, C])
        opw = sb("g_opw", [P, CH, C])
        dww = sb("g_dww", [P, CH, TAPS])
        dwb = sb("g_dwb", [P, CH])
        omb = sb("g_omb", [P, 27])
        vpb = sb("g_vpb", [P, CH])
        ones = sb("g_ones", [P, P])
        flag = sb("g_flag", [P, 1], mybir.dt.int32)
        ps = ctx.enter_context(nc.psum_tensor("g_ps", [P, 8, CT], F32))

        flag_summed, flag_made, loaded = sem("flag_summed"), sem("flag_made"), sem("g_loaded")
        with nc.Block() as block:
            @block.sync
            def _(sp):
                sp.dma_start(ones[:, :], w_dram["mean256"]).then_inc(loaded, 16)
                sp.wait_ge(loaded, 16)

            @block.tensor
            def _(pe):
                pe.wait_ge(loaded, 16)
                nc.tensor.matmul(ps[:, 0, 0:1], ones[:, :], reach[:, :], start=True, stop=True).then_inc(flag_summed, 1)

            @block.vector
            def _(dve):
                dve.wait_ge(flag_summed, 1)
                nc.vector.tensor_scalar(flag[:, :], ps[:, 0, 0:1], 0.0, None, ALU.is_gt).then_inc(flag_made, 1)
                dve.wait_ge(flag_made, 1)

        s_zero, s_zeroed, s_weights = sem("g_zero"), sem("g_zeroed"), sem("g_weights")
        x_in, x_normed_v, x_normed_d, v_bank, v_read = sem("g_x_in"), sem("g_nv"), sem("g_nd"), sem("g_vb"), sem("g_vr")
        v_ready, v_kept, xi_free = sem("g_v_ready"), sem("g_v_kept"), sem("g_xi_free")
        dw_step, om_bank, om_read = sem("g_dw_step"), sem("g_om_bank"), sem("g_om_read")
        rows_in, rows_used, acc_ready, acc_in = sem("g_rows_in"), sem("g_rows_used"), sem("g_acc_ready"), sem("g_acc_in")
        xres_in, pj_bank, pj_read = sem("g_xres_in"), sem("g_pj_bank"), sem("g_pj_read")
        x2_ready, x2_kept, x2_in, x2_used = sem("g_x2_ready"), sem("g_x2_kept"), sem("g_x2_in"), sem("g_x2_used")
        chain_a, pj_out, x_free = sem("g_chain_a"), sem("g_pj_out"), sem("g_x_free")
        gn_kept, chain, kept_dma = sem("g_gn_kept"), sem("g_chain"), sem("g_kept_dma")

        def take(eng, s, value):
            eng.wait_ge(s, value)
            eng.sem_clear(s)

        x_v = x.rearrange("n (h p) t -> n p h t", p=P)
        x2_v = x2.rearrange("n (h p) t -> n p h t", p=P)
        vpad_c = vpad.rearrange("(h p) y x -> p h y x", p=P)
        vpad_g = vpad.rearrange("(g c) y x -> g c y x", c=GC)
        of_image = lambda v, n: v[bass.ds(n, 1)].rearrange("n p h t -> p (n h) t")

        with nc.Block() as block:
            @block.sync
            def _(sp):
                with sp.If(sp.value_load(flag[0:1, 0:1], min_val=0, max_val=1) > 0):
                    for dst, name in ((dww, "dww"), (dwb, "dwb"), (omw, "omw"), (omb, "omb"), (vpw, "vpw_c"),
                                      (vpb, "vpb_c"), (opw, "opw")):
                        sp.dma_start(dst[:], w_dram[name]).then_inc(s_weights, 16)
                    sp.wait_ge(s_weights, 16 * 7)
                    take(sp, s_zero, 1)
                    zero = rows[:, :, :, :].rearrange("p c r x -> p (c r) x")
                    for h in range(CH):
                        for y in range(0, PADH, GC * SR):
                            k = min(GC * SR, PADH - y)
                            sp.dma_start(vpad_c[:, h, y:y + k, :], zero[:, 0:k, :]).then_inc(s_zeroed, 16)
                    sp.wait_ge(s_zeroed, 16 * CH * -(-PADH // (GC * SR)))
                    with sp.Fori(0, NI) as n:
                        sp.dma_start(xi[:, :, :], of_image(x_v, n)).then_inc(x_in, 16)
                        take(sp, v_ready, 1)
                        for h in range(CH):
                            sp.dma_start(vpad_c[:, h, R:R + H, R:R + W],
                                         xi[:, h, :].rearrange("p (r w) -> p r w", w=W)).then_inc(kept_dma, 16)
                        take(sp, kept_dma, 16 * CH)
                        sp.nop().then_inc(v_kept, 1)
                        with sp.Fori(0, STEPS) as j:
                            with sp.Fori(0, 2 * R + 1) as u:
                                take(sp, rows_used, 1)
                                for q in range(Q):
                                    sp.dma_start(rows[G * q:G * q + G, :, :, :],
                                                 vpad_g[:, :, bass.ds(j * SR + u + QR * q, SR), :]).then_inc(rows_in, 16)
                            take(sp, acc_ready, 1)
                            for q in range(Q):
                                for h in range(CH):
                                    g0 = G * q + h * (G // CH)
                                    sp.dma_start(acc_t[:, h, q * TOK:(q + 1) * TOK], acc[g0:g0 + G // CH, :, :])\
                                        .then_inc(kept_dma, 16)
                            take(sp, kept_dma, 16 * CH * Q)
                            sp.nop().then_inc(acc_in, 1)
                            for q in range(Q):
                                sp.dma_start(xres[:, :, q, :],
                                             of_image(x_v, n)[:, :, bass.ds(j * TOK + QR * W * q, TOK)]).then_inc(xres_in, 16)
                            take(sp, x2_ready, 1)
                            for q in range(Q):
                                sp.dma_start(of_image(x2_v, n)[:, :, bass.ds(j * TOK + QR * W * q, TOK)],
                                             xres[:, :, q, :]).then_inc(kept_dma, 16)
                            take(sp, kept_dma, 16 * Q)
                            sp.nop().then_inc(x2_kept, 1)
                        sp.dma_start(xi[:, :, :], of_image(x2_v, n)).then_inc(x2_in, 16)
                        take(sp, x2_used, 1)

            @block.scalar
            def _(act):
                with act.If(act.value_load(flag[0:1, 0:1], min_val=0, max_val=1) > 0):
                    act.wait_ge(s_weights, 16 * 7)
                    take(act, x_free, 1)
                    with act.Fori(0, NI) as n:
                        nc.scalar.activation(gn[:, :, :], tables[:, 0:2, bass.ds(n * CH, CH)], ACT.Copy).then_inc(gn_kept, 1)
                        take(act, gn_kept, 1)
                        take(act, x_in, 16)
                        for h in range(CH):
                            last = nc.scalar.activation(xpad[:, h, 1:1 + H, 1:1 + W],
                                                        xi[:, h, :].rearrange("p (r w) -> p r w", w=W), ACT.Identity,
                                                        bias=gn[:, 1, h:h + 1], scale=gn[:, 0, h:h + 1])
                            last.then_inc(x_normed_v, 1)
                        take(act, x_normed_v, CH)
                        nc.scalar.nop().then_inc(x_normed_d, 1)
                        nc.scalar.nop().then_inc(v_read, 1)
                        for u in range(CH * HW // CT):
                            h, t = u % CH, u // CH
                            take(act, v_bank, 1)
                            nc.scalar.activation(xi[:, h, CT * t:CT * t + CT], ps[:, 0, :], ACT.Identity,
                                                 bias=vpb[:, h:h + 1]).then_inc(chain_a, 1)
                            take(act, chain_a, 1)
                            nc.scalar.nop().then_inc(v_read if u + 1 < CH * HW // CT else v_ready, 1)
                        with act.Fori(0, STEPS) as j:
                            for u in range(4):
                                oh, tb = u // 2, u % 2
                                take(act, pj_bank, 1)
                                nc.scalar.activation(prj[:, oh, 2 * tb:2 * tb + 2, :], ps[:, 0, :].rearrange(
                                    "p (q t) -> p q t", q=2), ACT.Copy).then_inc(chain_a, 1)
                                take(act, chain_a, 1)
                                nc.scalar.nop().then_inc(pj_read if u < 3 else pj_out, 1)

            @block.tensor
            def _(pe):
                with pe.If(pe.value_load(flag[0:1, 0:1], min_val=0, max_val=1) > 0):
                    pe.wait_ge(s_weights, 16 * 7)
                    with pe.Fori(0, NI) as n:
                        for u in range(CH * HW // CT):
                            oh, t = u % CH, u // CH
                            take(pe, v_read, 1)
                            for h in range(CH):
                                mm = nc.tensor.matmul(ps[:, 0, :].rearrange("p (r w) -> p r w", w=W),
                                                      vpw[:, h, P * oh:P * oh + P],
                                                      xpad[:, h, 8 * t + 1:8 * t + 9, 1:1 + W],
                                                      start=h == 0, stop=h == CH - 1)
                            mm.then_inc(v_bank, 1)
                        with pe.Fori(0, STEPS) as j:
                            for u in range(27):
                                take(pe, dw_step if u == 0 else om_read, 1)
                                for h in range(CH):
                                    for q in range(Q):
                                        mm = nc.tensor.matmul(ps[G * q:G * q + G, 1, 0:TOK], omw[:, h, u, :],
                                                              xdw_step[:, h, q, :], start=h == 0, stop=h == CH - 1)
                                mm.then_inc(om_bank, 1)
                            for u in range(4):
                                oh, tb = u // 2, u % 2
                                take(pe, acc_in if u == 0 else pj_read, 1)
                                for h in range(CH):
                                    mm = nc.tensor.matmul(ps[:, 0, :], opw[:, h, P * oh:P * oh + P],
                                                          acc_t[:, h, CT * tb:CT * tb + CT],
                                                          start=h == 0, stop=h == CH - 1)
                                mm.then_inc(pj_bank, 1)

            @block.vector
            def _(dve):
                def link(ins):
                    ins.then_inc(chain, 1)
                    take(dve, chain, 1)

                with dve.If(dve.value_load(flag[0:1, 0:1], min_val=0, max_val=1) > 0):
                    link(nc.vector.memset(rows[:, :, :, :], 0.0))
                    nc.vector.nop().then_inc(s_zero, 1)
                    link(nc.vector.memset(xpad[:, :, :, :], 0.0))
                    dve.wait_ge(s_weights, 16 * 7)
                    dve.wait_ge(s_zeroed, 16 * CH * -(-PADH // (GC * SR)))
                    nc.vector.nop().then_inc(x_free, 1)
                    with dve.Fori(0, NI) as n:
                        take(dve, x_normed_d, 1)
                        for h in range(CH):
                            dst = xdw[:, h, :].rearrange("p (r w) -> p r w", w=W)
                            for k in range(TAPS):
                                src = xpad[:, h, k // 3:k // 3 + H, k % 3:k % 3 + W]
                                if k == 0:
                                    link(nc.vector.tensor_scalar(dst, src, dww[:, h, 0:1], dwb[:, h:h + 1],
                                                                 ALU.mult, ALU.add))
                                else:
                                    link(nc.vector.scalar_tensor_tensor(out=dst, in0=src, scalar=dww[:, h, k:k + 1],
                                                                        in1=dst, op0=ALU.mult, op1=ALU.add))
                        take(dve, v_kept, 1)
                        with dve.Fori(0, STEPS) as j:
                            for h in range(CH):
                                for q in range(Q):
                                    link(nc.vector.tensor_copy(xdw_step[:, h, q, :],
                                                               xdw[:, h, bass.ds(j * TOK + QR * W * q, TOK)]))
                            nc.vector.nop().then_inc(dw_step, 1)
                            for u in range(27):
                                take(dve, om_bank, 1)
                                if u < 2 * TAPS:
                                    k, axis = u // 2, u % 2
                                    shift = float((k % 3, k // 3)[axis] - 1)
                                    link(nc.vector.tensor_scalar(off[:, axis, k, :], ps[:, 1, 0:TOK], omb[:, u:u + 1],
                                                                 shift, ALU.add, ALU.add))
                                else:
                                    link(nc.vector.tensor_scalar(off[:, 2, u - 2 * TAPS, :], ps[:, 1, 0:TOK],
                                                                 omb[:, u:u + 1], None, ALU.add))
                                if u < 26:
                                    nc.vector.nop().then_inc(om_read, 1)
                            link(nc.vector.memset(acc[:, :, :], 0.0))
                            link(nc.vector.memset(at_y[:, :], float(-R)))
                            with dve.Fori(0, 2 * R + 1) as u:
                                nc.vector.nop().then_inc(rows_used, 1)
                                link(nc.vector.tensor_scalar(wy[:, :, :], off[:, 1, :, :], at_y[:, 0:1], None, ALU.subtract))
                                link(nc.vector.scalar_tensor_tensor(out=wy[:, :, :], in0=wy[:, :, :], scalar=-1.0,
                                                                    in1=wy[:, :, :], op0=ALU.mult, op1=ALU.max))
                                link(nc.vector.tensor_scalar(wy[:, :, :], wy[:, :, :], 1.0, -1.0, ALU.min, ALU.mult))
                                link(nc.vector.scalar_tensor_tensor(out=wy[:, :, :], in0=wy[:, :, :], scalar=1.0,
                                                                    in1=off[:, 2, :, :], op0=ALU.add, op1=ALU.mult))
                                link(nc.vector.tensor_scalar(at_y[:, :], at_y[:, :], 1.0, None, ALU.add))
                                link(nc.vector.memset(at_x[:, :], float(-R)))
                                take(dve, rows_in, 16 * Q)
                                with dve.Fori(0, 2 * R + 1) as v:
                                    link(nc.vector.tensor_scalar(wx[:, :, :], off[:, 0, :, :], at_x[:, 0:1], None, ALU.subtract))
                                    link(nc.vector.scalar_tensor_tensor(out=wx[:, :, :], in0=wx[:, :, :], scalar=-1.0,
                                                                        in1=wx[:, :, :], op0=ALU.mult, op1=ALU.max))
                                    link(nc.vector.tensor_scalar(wx[:, :, :], wx[:, :, :], 1.0, -1.0, ALU.min, ALU.mult))
                                    link(nc.vector.scalar_tensor_tensor(out=wx[:, :, :], in0=wx[:, :, :], scalar=1.0,
                                                                        in1=wy[:, :, :], op0=ALU.add, op1=ALU.mult))
                                    link(nc.vector.tensor_reduce(w[:, :], wx[:, :, :].rearrange("p k t -> p t k"),
                                                                 AX_X, ALU.add))
                                    link(nc.vector.tensor_tensor(
                                        tmp[:, :, :].rearrange("p c (r w) -> p c r w", w=W),
                                        rows[:, :, :, bass.ds(v, W)],
                                        w[:, :].rearrange("p (r w) -> p r w", w=W).unsqueeze(1)
                                        .to_broadcast([P, GC, SR, W]), ALU.mult))
                                    link(nc.vector.tensor_tensor(acc[:, :, :], acc[:, :, :], tmp[:, :, :], ALU.add))
                                    link(nc.vector.tensor_scalar(at_x[:, :], at_x[:, :], 1.0, None, ALU.add))
                            nc.vector.nop().then_inc(acc_ready, 1)
                            take(dve, pj_out, 1)
                            take(dve, xres_in, 16 * Q)
                            link(nc.vector.tensor_tensor(xres, xres, prj, ALU.add))
                            nc.vector.nop().then_inc(x2_ready, 1)
                            take(dve, x2_kept, 1)
                        take(dve, x2_in, 16)
                        for h in range(CH):
                            for i in range(HW // CT):
                                link(nc.vector.bn_stats(bs[:, h, i, :], xi[:, h, CT * i:CT * i + CT]))
                            link(nc.vector.bn_aggr(mv_now[:, h, :], bs[:, h, :, :]))
                        link(nc.vector.tensor_copy(mv2[:, bass.ds(n, 1), :, :].rearrange("p n h s -> p (n h s)"),
                                                   mv_now[:, :, :].rearrange("p h s -> p (h s)")))
                        nc.vector.nop().then_inc(x2_used, 1)


def layer1(nc, x2, w_dram, out, consts, tables, NI):
    CT = HW // 8
    CHUNKS = 8
    UNITS = CHUNKS * CH
    BANKS = 4
    PAD = H + 2
    with ExitStack() as ctx:
        sb = lambda name, shape, dt=F32: ctx.enter_context(nc.sbuf_tensor(name, shape, dt))
        sem = lambda name: ctx.enter_context(nc.semaphore(name))
        xb = sb("c_x", [P, 2, CH, HW])
        sgn = sb("c_sgn", [P, 2, CH, PAD, PAD], BF16)
        size = sb("c_size", [P, 2, CH, CT])
        beta = sb("c_beta", [P, PAD, PAD])
        hsum = sb("c_hsum", [P, PAD, W])
        box = sb("c_box", [P, 2, H, W])
        kern = box[:, :, :, :].rearrange("p b r w -> p (b r w)")[:, 0:CH * TAPS * C]\
            .rearrange("p (h k c) -> p h k c", h=CH, k=TAPS)
        ksgn = sb("c_ksgn", [P, CH, TAPS, C], BF16)
        res = sb("c_res", [P, BANKS, CT])
        mean256 = sb("c_mean", [P, P])
        bias = sb("c_bias", [P, CH])
        scale = sb("c_scale", [P, CH])
        gn = sb("c_gn", [P, 2, 2, CH])
        gn_kept = sem("c_gn_kept")
        ps_c = [ctx.enter_context(nc.psum_tensor(f"ps_c{i}", [P, 8, W], F32)) for i in range(BANKS)]
        ps_b = [ctx.enter_context(nc.psum_tensor(f"ps_b{i}", [P, 8, W], F32)) for i in range(2)]
        ps_alpha = ctx.enter_context(nc.psum_tensor("ps_alpha", [P, 512], F32))

        consts_loaded, kern_loaded = sem("c_consts"), sem("kern_loaded")
        kern_signed, kern_sized, alpha_part = sem("kern_signed"), sem("kern_sized"), sem("alpha_part")
        scale_made, cleared = sem("scale_made"), sem("cleared")
        x_loaded = [sem(f"c_loaded{b}") for b in range(2)]
        signed, sized, halves_added = sem("signed"), sem("sized"), sem("halves_added")
        beta_full, beta_out = sem("beta_full"), sem("beta_out")
        hsum_done, box_half, box_done = sem("hsum_done"), sem("box_half"), sem("box_done")
        conv_full, mult_done, affine_done, added = sem("conv_full"), sem("mult_done"), sem("affine_done"), sem("added")
        stored = sem("stored")
        QUARTERS = 4

        def images(eng, image):
            for b in range(2):
                image(b, b, False)
            if NI > 4:
                with eng.Fori(1, NI // 2 - 1) as m:
                    for b in range(2):
                        image(2 * m + b, b, False)
            for b in range(2):
                image(NI - 2 + b, b, b == 1)

        def of_image(v, n):
            return v[n] if isinstance(n, int) else v[bass.ds(n, 1)].rearrange("n p h t -> p (n h) t")

        x2_v = x2.rearrange("n (h p) t -> n p h t", p=P)
        out_v = out.rearrange("n (h p) t -> n p h t", p=P)

        def pair(n, b):
            return n // 2 if isinstance(n, int) else (n - b) // 2

        with nc.Block() as block:
            @block.sync
            def _(sp):
                sp.dma_start(mean256[:, :], w_dram["mean256"]).then_inc(consts_loaded, 16)
                sp.dma_start(bias[:, :], w_dram["bias"]).then_inc(consts_loaded, 16)
                sp.dma_start(kern, w_dram["kernel"]).then_inc(kern_loaded, 16)
                for b in range(2):
                    sp.dma_start(xb[:, b, :, :], x2_v[b]).then_inc(x_loaded[b], 16)

                def image(n, b, last):
                    for i in range(QUARTERS):
                        sp.wait_ge(added, UNITS * n + UNITS // QUARTERS * (i + 1))
                        at = slice(HW // QUARTERS * i, HW // QUARTERS * (i + 1))
                        sp.dma_start(of_image(out_v, n)[:, :, at], xb[:, b, :, at]).then_inc(stored, 16)
                    if isinstance(n, int) and n + 2 >= NI:
                        return
                    sp.wait_ge(stored, 16 * QUARTERS * (n + 1))
                    sp.dma_start(xb[:, b, :, :], of_image(x2_v, n + 2)).then_inc(x_loaded[b], 16)

                images(sp, image)
                sp.wait_ge(stored, 16 * QUARTERS * NI)

            @block.scalar
            def _(act):
                act.wait_ge(kern_signed, CH)
                for h in range(CH):
                    nc.scalar.activation(kern[:, h], kern[:, h], ACT.Abs).then_inc(kern_sized, 1)
                act.wait_ge(cleared, 1)
                act.wait_ge(consts_loaded, 32)

                def sizes(n, b, t):
                    i = CHUNKS * n + t
                    if t == 0:
                        nc.scalar.activation(gn[:, b, :, :], tables[:, 0:2, bass.ds(n * CH, CH)], ACT.Copy)\
                            .then_inc(gn_kept, 1)
                        act.wait_ge(gn_kept, n + 1)
                        act.wait_ge(x_loaded[b], 16 * (pair_of[0] + 1))
                    if not isinstance(i, int) or i > 1:
                        act.wait_ge(beta_full, i - 1)
                    for h in range(CH):
                        last = nc.scalar.activation(size[:, t % 2, h, :], xb[:, b, h, CT * t:CT * t + CT], ACT.Abs,
                                                    bias=gn[:, b, 1, h:h + 1], scale=gn[:, b, 0, h:h + 1])
                    last.then_inc(sized, 1)

                def keep_beta(n, t):
                    act.wait_ge(beta_full, CHUNKS * n + t + 1)
                    at_least(act, box_done, CHUNKS * n)
                    nc.scalar.activation(beta[:, 8 * t + 1:8 * t + 9, 1:1 + W], ps_b[t % 2][:, :, :], ACT.Copy)\
                        .then_inc(beta_out, 1)

                pair_of = [0]
                for t in range(CHUNKS):
                    sizes(0, 0, t)
                    if t > 0:
                        keep_beta(0, t - 1)
                keep_beta(0, CHUNKS - 1)

                def image(n, b, last):
                    pair_of[0] = pair(n, b) + b
                    for u in range(UNITS):
                        t = u - UNITS // 2
                        if t >= 0 and not last:
                            sizes(n + 1, 1 - b, t)
                        act.wait_ge(mult_done, UNITS * n + u + 1)
                        v = res[:, u % BANKS, :]
                        nc.scalar.activation(v, v, ACT.Identity, bias=bias[:, u % CH:u % CH + 1],
                                             scale=scale[:, u % CH:u % CH + 1]).then_inc(affine_done, 1)
                        if t >= 1 and not last:
                            keep_beta(n + 1, t - 1)
                    if not last:
                        keep_beta(n + 1, CHUNKS - 1)

                act.wait_ge(scale_made, 1)
                images(act, image)

            @block.tensor
            def _(pe):
                pe.wait_ge(consts_loaded, 32)
                pe.wait_ge(kern_sized, CH)
                for oh in range(CH):
                    for i in range(CH * TAPS):
                        h, k = i // TAPS, i % TAPS
                        mm = nc.tensor.matmul(ps_alpha[:, oh:oh + 1], kern[:, h, k, P * oh:P * oh + P],
                                              mean256[:, 0:1], start=i == 0, stop=i == CH * TAPS - 1)
                mm.then_inc(alpha_part, 1)

                def mean_size(n, t):
                    i = CHUNKS * n + t
                    pe.wait_ge(halves_added, i + 1)
                    if not isinstance(i, int) or i > 1:
                        pe.wait_ge(beta_out, i - 1)
                    nc.tensor.matmul(ps_b[t % 2][:, :, :], mean256[:, :], size[:, t % 2, 0, :],
                                     start=True, stop=True).then_inc(beta_full, 1)

                def convolve(n, b, u):
                    t, oh = u // CH, u % CH
                    i = UNITS * n + u
                    if not isinstance(i, int) or i >= BANKS:
                        pe.wait_ge(mult_done, i - BANKS + 1)
                    for h in range(CH):
                        for k in range(TAPS):
                            ky, kx = k // 3, k % 3
                            mm = nc.tensor.matmul(
                                ps_c[u % BANKS][:, :, :], ksgn[:, h, k, P * oh:P * oh + P],
                                sgn[:, b, h, 8 * t + ky:8 * t + ky + 8, kx:kx + W],
                                start=h == 0 and k == 0, stop=h == CH - 1 and k == TAPS - 1)
                    mm.then_inc(conv_full, 1)

                pe.wait_ge(signed, CH)
                for t in range(CHUNKS):
                    mean_size(0, t)
                    if t % 2 == 1:
                        convolve(0, 0, t // 2)

                def image(n, b, last):
                    pe.wait_ge(signed, CH * (n + 1))
                    for u in range(BANKS if isinstance(n, int) and n == 0 else 0, UNITS):
                        convolve(n, b, u)
                        if u >= UNITS // 2 and not last:
                            mean_size(n + 1, u - UNITS // 2)

                images(pe, image)

            @block.gpsimd
            def _(pool):
                def image(n, b, last):
                    for u in range(UNITS):
                        t, oh = u // CH, u % CH
                        pool.wait_ge(affine_done, UNITS * n + u + 1)
                        v = xb[:, b, oh, CT * t:CT * t + CT]
                        nc.gpsimd.tensor_tensor(v, v, res[:, u % BANKS, :], ALU.add).then_inc(added, 1)

                images(pool, image)

            @block.vector
            def _(dve):
                for r in (0, PAD - 1):
                    nc.vector.memset(sgn[:, :, :, r, :].rearrange("p b h w -> p (b h) w"), -0.5)
                    nc.vector.memset(sgn[:, :, :, 1:PAD - 1, r], -0.5)
                    nc.vector.memset(beta[:, r, :], 0.0)
                    nc.vector.memset(beta[:, 1:PAD - 1, r], 0.0)
                    last = nc.vector.memset(hsum[:, r, :], 0.0)
                last.then_inc(cleared, 1)
                dve.wait_ge(cleared, 1)
                dve.wait_ge(kern_loaded, 16)
                for h in range(CH):
                    nc.vector.tensor_scalar(ksgn[:, h, :, :], kern[:, h], 0.0, 0.5, ALU.is_gt, ALU.subtract)\
                        .then_inc(kern_signed, 1)

                def add_halves(n, t):
                    dve.wait_ge(sized, CHUNKS * n + t + 1)
                    nc.vector.tensor_tensor(size[:, t % 2, 0, :], size[:, t % 2, 0, :], size[:, t % 2, 1, :], ALU.add)\
                        .then_inc(halves_added, 1)

                def across(n, t):
                    dve.wait_ge(beta_out, CHUNKS * n + t + 1)
                    at_least(dve, box_done, CHUNKS * n)
                    r = slice(8 * t + 1, 8 * t + 9)
                    nc.vector.tensor_tensor(hsum[:, r, :], beta[:, r, 0:W], beta[:, r, 1:1 + W], ALU.add)\
                        .then_inc(hsum_done, 1)
                    dve.wait_ge(hsum_done, 2 * (CHUNKS * n + t) + 1)
                    nc.vector.tensor_tensor(hsum[:, r, :], hsum[:, r, :], beta[:, r, 2:2 + W], ALU.add)\
                        .then_inc(hsum_done, 1)

                def down(n, b, t):
                    i = CHUNKS * n + t
                    dve.wait_ge(hsum_done, 2 * (CHUNKS * n + min(t + 2, CHUNKS)))
                    if not isinstance(n, int) or n > 1:
                        dve.wait_ge(mult_done, UNITS * (n - 1))
                    dst = box[:, b, 8 * t:8 * t + 8, :]
                    nc.vector.tensor_tensor(dst, hsum[:, 8 * t:8 * t + 8, :], hsum[:, 8 * t + 1:8 * t + 9, :], ALU.add)\
                        .then_inc(box_half, 1)
                    dve.wait_ge(box_half, i + 1)
                    nc.vector.tensor_tensor(dst, dst, hsum[:, 8 * t + 2:8 * t + 10, :], ALU.add).then_inc(box_done, 1)

                def signs(n, b, m):
                    dve.wait_ge(x_loaded[b], 16 * (m + 1))
                    if not isinstance(n, int) or n > 1:
                        dve.wait_ge(conv_full, UNITS * (n - 1))
                    for h in range(CH):
                        mean = tables[:, 2, bass.ds(n * CH + h, 1)]
                        nc.vector.tensor_scalar(sgn[:, b, h, 1:1 + H, 1:1 + W],
                                                xb[:, b, h, :].rearrange("p (r w) -> p r w", w=W), mean, 0.5,
                                                ALU.is_gt, ALU.subtract).then_inc(signed, 1)

                signs(0, 0, 0)
                add_halves(0, 0)
                dve.wait_ge(alpha_part, 1)
                nc.vector.tensor_scalar(scale[:, :], ps_alpha[:, 0:CH], 4.0 / (TAPS * TAPS), None, ALU.mult)\
                    .then_inc(scale_made, 1)
                for t in range(CHUNKS):
                    if t + 1 < CHUNKS:
                        add_halves(0, t + 1)
                    across(0, t)
                    if t > 0:
                        down(0, 0, t - 1)
                down(0, 0, CHUNKS - 1)

                def image(n, b, last):
                    for u in range(UNITS):
                        t = u // CH
                        i = UNITS * n + u
                        if u == UNITS // 2 and not last:
                            signs(n + 1, 1 - b, pair(n, b) + b)
                        if u >= UNITS // 2 and not last:
                            add_halves(n + 1, u - UNITS // 2)
                        dve.wait_ge(conv_full, i + 1)
                        dve.wait_ge(box_done, CHUNKS * n + t + 1)
                        if not isinstance(i, int) or i >= BANKS:
                            dve.wait_ge(added, i - BANKS + 1)
                        nc.vector.tensor_tensor(res[:, u % BANKS, :].rearrange("p (r w) -> p r w", w=W),
                                                ps_c[u % BANKS][:, :, :], box[:, b, 8 * t:8 * t + 8, :], ALU.mult)\
                            .then_inc(mult_done, 1)
                        t = u - UNITS // 2
                        if t >= 1 and not last:
                            across(n + 1, t - 1)
                        if t >= 2 and not last:
                            down(n + 1, 1 - b, t - 2)
                    if not last:
                        across(n + 1, CHUNKS - 1)
                        down(n + 1, 1 - b, CHUNKS - 2)
                        down(n + 1, 1 - b, CHUNKS - 1)

                images(dve, image)


def layout(inputs, NI=8):
    f = lambda name: np.asarray(inputs[name])
    halves = lambda a: np.ascontiguousarray(a.reshape((CH, P) + a.shape[1:]).swapaxes(0, 1))
    per_block = lambda a: np.ascontiguousarray(np.tile(a, (Q, 1)))
    mean8 = np.kron(np.eye(P // GC), np.full((GC, GC), 1.0 / GC)).astype(np.float32)
    return {
        "x": np.ascontiguousarray(f("x")[:NI].reshape(NI, HW, C).swapaxes(1, 2)),
        "dww": halves(f("L0_conv_dw_w").reshape(TAPS, C).T),
        "dww3": np.pad(f("L0_conv_dw_w").reshape(3, 3, CH, CB, 32).transpose(0, 4, 2, 3, 1)
                       .reshape(KROWS, CH, CB, 3), ((0, P - KROWS), (0, 0), (0, 0), (0, 0))),
        "eye3": np.pad(np.tile(np.eye(32, dtype=np.float32), (3, 1)), ((0, P - KROWS), (0, 0))),
        "dwb": halves(f("L0_conv_dw_b")),
        "omw": halves(f("L0_conv_om_w").reshape(C, G, 27).swapaxes(1, 2)),
        "omb": per_block(f("L0_conv_om_b").reshape(G, 27)),
        "vpw": halves(f("L0_conv_vp_w").reshape(C, G, GC).swapaxes(1, 2)),
        "vpb": per_block(f("L0_conv_vp_b").reshape(G, GC)),
        "opw": halves(f("L0_conv_op_w")),
        "vpw_c": halves(f("L0_conv_vp_w")),
        "vpb_c": halves(f("L0_conv_vp_b")),
        "kernel": halves(f("L1_conv_kernel").reshape(TAPS, C, C).swapaxes(0, 1)),
        "bias": halves(f("L1_conv_bias")),
        "ident": np.eye(P, dtype=np.float32),
        "mean8": mean8,
        "mean256": np.full((P, P), 1.0 / C, np.float32),
        "zeros": np.zeros((P, CH, 2, W), np.float32),
    }


def program(nc, d, out, NI=8):
    x2 = nc.dram_tensor("x2", (NI, C, HW), F32, kind="Internal").ap()
    with ExitStack() as ctx:
        sb = lambda name, shape, dt=F32: ctx.enter_context(nc.sbuf_tensor(name, shape, dt))
        consts = {"ident": sb("ident", [P, P]), "mean8": sb("mean8", [P, P]),
                  "minus1": sb("minus1", [P, 1]), "scratch": sb("scratch", [P, 2])}
        tables = sb("tables", [P, 3, NI * CH])
        mv2 = sb("mv2", [P, NI, CH, 2])
        reach = sb("reach", [P, 1])
        setup = ctx.enter_context(nc.semaphore("setup"))
        setup_v = ctx.enter_context(nc.semaphore("setup_v"))
        with nc.Block() as block:
            @block.sync
            def _(sp):
                sp.dma_start(consts["mean8"][:, :], d["mean8"]).then_inc(setup, 16)
                sp.wait_ge(setup, 16)

            @block.vector
            def _(dve):
                nc.vector.memset(consts["minus1"][:, :], -1.0).then_inc(setup_v, 1)
                dve.wait_ge(setup_v, 1)
        first_stats(nc, d["x"], consts, tables[:, :, 0:CH])
        layer0(nc, d["x"], d["zeros"], d, x2, consts, tables, mv2, reach, NI)
        layer0_any_offset(nc, d["x"], d, x2, consts, tables, mv2, reach, NI)
        group_tables(nc, mv2, consts, tables, NI, "gt2_")
        layer1(nc, x2, d, out, consts, tables, NI)



def kernel(**inputs):
    import concourse.bacc as _bacc
    from concourse.bass_utils import run_bass_kernel_spmd as _run

    nc = _bacc.Bacc("TRN2", target_bir_lowering=False, num_devices=1)
    arrays, d = {}, {}
    for name, a in layout(inputs).items():
        arrays[f"in_{name}_dram"] = a
        d[name] = nc.dram_tensor(f"in_{name}_dram", a.shape, mybir.dt.from_np(a.dtype), kind="ExternalInput").ap()
    n = inputs["x"].shape[0]
    out = nc.dram_tensor("out_0_dram", (n, C, HW), F32, kind="ExternalOutput").ap()
    program(nc, d, out, n)
    r = _run(nc, [arrays], core_ids=[0])
    got = r.results[0]["out_0_dram"]
    return np.ascontiguousarray(got.reshape(n, C, H, W).transpose(0, 2, 3, 1))
```
